# Optimizing a Trainium2 kernel written in Bass

```python
import numpy as np
import jax
import jax.numpy as jnp

def _softmax(x, axis=-1):
    return jax.nn.softmax(x, axis=axis)

def _gelu(x):
    return jax.nn.gelu(x, approximate=True)

def _silu(x):
    return jax.nn.silu(x)

def _sigmoid(x):
    return jax.nn.sigmoid(x)

def _layernorm(x, axis=-1, eps=1e-05):
    m = jnp.mean(x, axis=axis, keepdims=True)
    v = jnp.var(x, axis=axis, keepdims=True)
    return (x - m) / jnp.sqrt(v + eps)

def _scatter_add(tgt, idx, src, axis=0):
    return tgt.at[idx].add(src)

def _segment_sum(src, seg, n):
    return jax.ops.segment_sum(src, seg, n)
kernel_name = 'mk_gnn_resnorm_d2_gnn_r32_673f43'

def setup_inputs(seed: int=0):
    np.random.seed(seed)
    _w = jnp.asarray

    def _rec_inputs():
        import jax
        import jax.numpy as jnp
        _gk = jax.random.key(seed)
        x = 0.5001 + 0.2887 * jax.random.normal(jax.random.fold_in(_gk, 1), (3125, 128), jnp.float32)
        _s = jax.random.randint(jax.random.fold_in(_gk, 2), (50000,), 0, 3125, jnp.int32)
        _d = jax.random.randint(jax.random.fold_in(_gk, 3), (50000,), 0, 3125, jnp.int32)
        _loop = jnp.arange(3125, dtype=jnp.int32)
        src = jnp.concatenate([_s, _d, _loop])
        dst = jnp.concatenate([_d, _s, _loop])
        _o = jnp.argsort(dst, stable=True)
        src = src[_o]
        dst = dst[_o]
        edge_type_9 = jax.random.randint(jax.random.fold_in(_gk, 12), (103125,), 0, 9, jnp.int32)
        return (x, src, dst, edge_type_9)
    x, src, dst, edge_type_9 = _rec_inputs()

    def _L0_gnn_setup():
        import jax, jax.numpy as jnp
        import numpy as np
        N_NODES = 50000
        HIDDEN = 128
        N_REL = 9
        N_LAYERS = 3
        N_EDGES = 18750
        key = jax.random.key(seed)
        k1, k2, k3, k4, k5 = jax.random.split(key, 5)
        edge_index = jax.random.randint(k1, (2, N_EDGES), 0, N_NODES, dtype=jnp.int64 if jax.config.jax_enable_x64 else jnp.int32)
        edge_type = jax.random.randint(k2, (N_EDGES,), 0, N_REL, dtype=edge_index.dtype)
        embeddings = jax.random.uniform(k3, (N_NODES, HIDDEN), dtype=jnp.float32)
        weights = jax.random.uniform(k4, (N_LAYERS, N_REL, HIDDEN, HIDDEN), dtype=jnp.float32)
        biases = jax.random.uniform(k5, (N_LAYERS, N_REL, HIDDEN), dtype=jnp.float32)
        return {'edge_index': edge_index, 'edge_type': edge_type, 'embeddings': embeddings, 'weights': weights, 'biases': biases}
    _L0_gnn_all = _L0_gnn_setup()
    _L0_gnn_in = {k: v for k, v in _L0_gnn_all.items() if k in ('weights', 'biases')}
    del _L0_gnn_all

    def _L1_gnn_setup():
        import jax, jax.numpy as jnp
        import numpy as np
        N_NODES = 1250
        N_EDGES = 20000
        D_FEAT = 128
        key = jax.random.key(seed)
        k1, k2, k3, k4 = jax.random.split(key, 4)
        x = jax.random.normal(k1, (N_NODES, D_FEAT), dtype=jnp.float32)
        beta = jax.random.uniform(k2, (1,), dtype=jnp.float32)
        row = jax.random.randint(k3, (N_EDGES,), 0, N_NODES)
        col = (row + 1 + jax.random.randint(k4, (N_EDGES,), 0, N_NODES - 1)) % N_NODES
        edge_index = jnp.stack([row, col]).astype(jnp.int64)
        return {'x': x, 'beta': beta, 'edge_index': edge_index}
    _L1_gnn_all = _L1_gnn_setup()
    _L1_gnn_in = {k: v for k, v in _L1_gnn_all.items() if k in ('beta',)}
    del _L1_gnn_all
    return {'x': x, 'src': src, 'dst': dst, 'edge_type_9': edge_type_9, 'L0_gnn_weights': _L0_gnn_in['weights'], 'L0_gnn_biases': _L0_gnn_in['biases'], 'L1_gnn_beta': _L1_gnn_in['beta']}

def reference(x, src, dst, edge_type_9, L0_gnn_weights, L0_gnn_biases, L1_gnn_beta):
    import jax
    import jax.numpy as jnp

    def _L0_gnn_ref(edge_index, edge_type, embeddings, weights, biases):
        import jax, jax.numpy as jnp
        import numpy as np
        N_NODES = 50000
        HIDDEN = 128
        N_REL = 9
        N_LAYERS = 3
        N_EDGES = 18750
        L = weights.shape[0]
        N = embeddings.shape[0]
        dest = edge_index[0]
        src = edge_index[1]
        out = embeddings
        for l in range(L):
            X = jnp.einsum('ne,ref->rnf', out, weights[l])
            msg = X[edge_type, src] + biases[l][edge_type]
            hidden = jax.ops.segment_sum(msg, dest, num_segments=N)
            if l + 1 < L:
                hidden = jax.nn.relu(hidden)
            out = hidden
        return out

    def _L1_gnn_ref(x, beta, edge_index):
        import jax, jax.numpy as jnp
        import numpy as np
        N_NODES = 1250
        N_EDGES = 20000
        D_FEAT = 128
        num_nodes = x.shape[0]
        row, col = (edge_index[0], edge_index[1])
        loop = jnp.arange(num_nodes, dtype=row.dtype)
        row = jnp.concatenate([row, loop])
        col = jnp.concatenate([col, loop])
        norm = jnp.linalg.norm(x, axis=1)
        alpha = jnp.sum(x[row] * x[col], axis=1) / (norm[row] * norm[col])
        alpha = alpha * beta[0]
        amax = jax.ops.segment_max(alpha, row, num_segments=num_nodes)
        alpha = jnp.exp(alpha - amax[row])
        denom = jax.ops.segment_sum(alpha, row, num_segments=num_nodes)
        alpha = alpha / denom[row]
        out = jax.ops.segment_sum(alpha[:, None] * x[col], row, num_segments=num_nodes)
        return out
    edge_index = jnp.stack([src, dst])
    x = _layernorm(x + _L0_gnn_ref(edge_index, edge_type_9, x, L0_gnn_weights, L0_gnn_biases), axis=-1)
    x = _layernorm(x + _L1_gnn_ref(x, L1_gnn_beta, edge_index), axis=-1)
    return x

_drawn_inputs = setup_inputs


def setup_inputs(seed=0):
    import zlib

    import numpy as np

    out = dict(_drawn_inputs(seed))
    spreads = {}
    factors = {}
    for name, (base, spread) in spreads.items():
        noise = np.random.default_rng([zlib.crc32(name.encode()), seed]).standard_normal(out[name].shape)
        drawn = base * np.exp(spread * noise) if base else spread * noise
        out[name] = jnp.asarray(drawn.astype(out[name].dtype))
    for name, factor in factors.items():
        out[name] = (out[name] * factor).astype(out[name].dtype)
    return out
```

```python
from contextlib import ExitStack

import concourse.bass as bass
from concourse import mybir

F32 = mybir.dt.float32
BF16 = mybir.dt.bfloat16
I32 = mybir.dt.int32
I16 = mybir.dt.int16
ALU = mybir.AluOpType
ACT = mybir.ActivationFunctionType
AX = mybir.AxisListType

P = 128
U = 8
HALF = U // 2
BIG = 1.0e30
EPS = 1e-05
NO_ROW = 999


def gnn_program(nc, x, src, dst, edge_type, weights, biases, beta, out):
    N, D = x.shape
    E = src.shape[0]
    L, R = weights.shape[0], weights.shape[1]
    NB = -(-N // P)
    NP = NB * P
    LAST = N - (NB - 1) * P
    RF = R * D
    ET = -(-E // (P * U)) * U
    FULL = E // ET
    REST = E - FULL * ET
    assert D == P and FULL == P - 1
    NK = NB + 1
    PAD_ROW = NB * P
    NT = -(-(E // P + NB) // U) * U
    TW = NT + U
    SLACK = P * ET - E
    assert (E + NB * (P - 1)) // P <= NT and (E + NB * (P - 1)) // P + -(-SLACK // P) <= TW
    PAYS = 4
    HL = 2 * D + 4
    G3 = 3 * D
    XC = RF // G3
    XB = 5
    XU = 5
    assert NB % XU == 0 and RF % G3 == 0

    table = nc.dram_tensor("sorted_edges", (P * TW, PAYS), I32, kind="Internal").ap()
    xt = nc.dram_tensor("x_of_type", (R * NP, D), F32, kind="Internal").ap()
    yt = nc.dram_tensor("attended_rows", (NP, HL), F32, kind="Internal").ap()

    with ExitStack() as ctx:
        def sb(name, shape, dt=F32):
            return ctx.enter_context(nc.sbuf_tensor(name, shape, dt))

        def sem(name):
            return ctx.enter_context(nc.semaphore(name))

        nodes = sb("nodes", [P, NB, D])
        wsb = sb("wsb", [P, L * R, D])
        bias = sb("bias", [P, L * RF])
        hT = sb("hT", [P, NP])
        ident = sb("ident", [P, P])
        identb = sb("identb", [P, P], BF16)
        zerob = sb("zerob", [P, 512], BF16)
        iota_r = sb("iota_r", [P, P])
        srt = sb("srt", [P, TW, PAYS], I32)
        rowf = sb("rowf", [P, TW])
        blk = sb("blk", [P, TW])
        blki = sb("blki", [P, TW], I32)
        betab = sb("betab", [P, 1])
        idx = sb("idx", [P, U], I32)
        oh = sb("oh", [P, U, P])
        sm = sb("sm", [P, 12, NK])
        smi = sb("smi", [P, 2, NK], I32)

        REGION = 27 * 1024
        region = sb("region", [P, REGION])
        used = [0]

        def part(words, dt=F32):
            a = region[:, used[0]:used[0] + words]
            used[0] += words
            assert used[0] <= REGION, used[0]
            return a if dt == F32 else a.bitcast(dt)

        eq = part(NK * ET // 2, BF16).rearrange("p (b t) -> p b t", b=NK)
        cum = part(NK * ET // 2, I16).rearrange("p (b t) -> p b t", b=NK)
        pay = part(ET * (PAYS + 1), I32).rearrange("p (t w) -> p t w", w=PAYS + 1)
        sring = part(U * (PAYS + 1), I32).rearrange("p (t w) -> p t w", w=PAYS + 1)
        keyb = part(ET // 2, BF16)
        pos = part(ET)
        posi = part(ET, I32)
        tmp, tmpi = blk[:, 0:ET], blki[:, 0:ET]
        srci, dsti, typei = (hT[:, n * ET:(n + 1) * ET].bitcast(I32) for n in range(3))
        used[0] = 0
        grow = part(U * D).rearrange("p (u d) -> p u d", u=U)
        hblk = part(XU * P).rearrange("p (u d) -> p u d", u=XU)
        xst = part(XU * RF).rearrange("p (u w) -> p u w", u=XU)
        used[0] = 0
        gat = part(U * HL).rearrange("p (u w) -> p u w", u=U)
        rows = part(NB * HL).rearrange("p (b w) -> p b w", b=NB)
        acc = part(NB * (D + 1)).rearrange("p (b w) -> p b w", b=NB)
        gt = part(2 * P).rearrange("p (s w) -> p s w", s=2)
        yb = part(2 * P).rearrange("p (s w) -> p s w", s=2)
        neg = part(P, BF16).rearrange("p (s w) -> p s w", s=2)
        pr = part(2 * P).rearrange("p (s w) -> p s w", s=2)
        pt = part(2 * P).rearrange("p (s w) -> p s w", s=2)
        nmn = part(4)
        nold = part(4)
        scl = part(4)
        tmx = part(4)
        fin = part(NB * D).rearrange("p (b w) -> p b w", b=NB)
        sq = part(D)
        ltri, ones = oh[:, 0, :], oh[:, 1, :]

        stats = sb("stats", [P, NB, 6])
        mv = sb("mv", [P, NB, 2])
        nm = sb("nm", [P, NB])

        ps = ctx.enter_context(nc.psum_tensor("ps", [P, 8, 512], F32))
        agg = ps[:, 0:7, :].rearrange("p k n -> p (k n)")

        s_edges = sem("s_edges")
        s_const = sem("s_const")
        s_pool = sem("s_pool")
        s_d = sem("s_d")
        s_a = sem("s_a")
        s_t = sem("s_t")
        s_fill = sem("s_fill")
        s_sidx = sem("s_sidx")
        s_scat = [sem(f"s_scat{u}") for u in range(U)]
        s_srt = sem("s_srt")
        s_hb = sem("s_hb")
        s_xm = sem("s_xm")
        s_xe = sem("s_xe")
        s_xd = [sem(f"s_xd{u}") for u in range(XU)]
        s_idx = sem("s_idx")
        s_g = [sem(f"s_g{u}") for u in range(U)]
        s_oh = sem("s_oh")
        s_used = sem("s_used")
        s_yt = sem("s_yt")
        s_tr = sem("s_tr")
        s_gt = sem("s_gt")
        s_ny = sem("s_ny")
        s_sc = sem("s_sc")
        s_mx = sem("s_mx")
        s_nm = sem("s_nm")
        s_no = sem("s_no")
        s_up = sem("s_up")
        s_ex = sem("s_ex")
        s_pt = sem("s_pt")
        s_pc = sem("s_pc")
        s_pv = sem("s_pv")
        s_ac = sem("s_ac")
        s_out = sem("s_out")

        marks = {}

        block = ctx.enter_context(nc.Block())

        def reg_wait(eng, s, value):
            eng.wait_ge(s, value)
            eng.nop(nofuse=True)

        @block.vector
        def _(dve):
            steps = [0]

            def step(ins, mark=None):
                steps[0] += 1
                ins.then_inc(s_d, 1)
                dve.wait_ge(s_d, steps[0])
                if mark:
                    marks[mark] = steps[0]

            dve.sem_inc(s_used, U)
            dve.sem_inc(s_pv, U)
            dve.sem_inc(s_xe, XB)
            dve.sem_inc(s_xm, XU * XC)
            nc_ = dve
            step(nc_.memset(srci, PAD_ROW))
            step(nc_.memset(dsti, 0))
            step(nc_.memset(typei, 0), "cleared")
            nc_.memset(zerob[:, :], 0.0)
            step(nc_.memset(srt[:, :, :], 0))
            step(nc_.memset(srt[:, :, 2:3], NO_ROW), "filler")

            dve.wait_ge(s_edges, 96)
            step(nc_.tensor_scalar(tmpi, srci, 7, None, ALU.arith_shift_right))
            step(nc_.tensor_copy(keyb, tmpi))
            step(nc_.tensor_scalar(posi, tmpi, float(NB - 1), -float(P), ALU.min, ALU.mult))
            step(nc_.tensor_tensor(pay[:, :, 2:3].rearrange("p t w -> p (t w)"), srci, posi, ALU.add))
            step(nc_.tensor_copy(pay[:, :, 1:2].rearrange("p t w -> p (t w)"), dsti))
            step(nc_.memset(pay[:, :, 3:4], 0))
            step(nc_.scalar_tensor_tensor(out=pay[:, :, 0:1].rearrange("p t w -> p (t w)"), in0=typei,
                                          scalar=float(NP), in1=dsti, op0=ALU.mult, op1=ALU.add))
            for b in range(NK):
                ins = nc_.tensor_scalar(eq[:, b, :], keyb, float(b), None, ALU.is_equal)
            step(ins)
            eqf = eq.rearrange("p b t -> p (b t)")
            step(nc_.tensor_tensor_scan(cum.rearrange("p b t -> p (b t)"), eqf, eqf, 0.0,
                                        ALU.add, ALU.bypass))
            ends, cnt, prev, pre, tot, til, te, ts, off = (sm[:, i, :] for i in range(9))
            step(nc_.tensor_copy(ends, cum[:, :, ET - 1]))
            step(nc_.memset(prev[:, 0:1], 0.0))
            step(nc_.tensor_copy(prev[:, 1:NK], ends[:, 0:NK - 1]))
            step(nc_.tensor_tensor(cnt, ends, prev, ALU.subtract), "counts")
            dve.wait_ge(s_t, 2)
            step(nc_.tensor_copy(pre, ps[:, 0, 0:NK]))
            step(nc_.tensor_copy(tot, ps[:, 1, 0:NK]), "totals")
            step(nc_.tensor_scalar(tot, tot, float(P - 1), None, ALU.add))
            step(nc_.tensor_copy(smi[:, 0, :], tot))
            step(nc_.tensor_scalar(smi[:, 1, :], smi[:, 0, :], 7, None, ALU.arith_shift_right))
            step(nc_.tensor_copy(til, smi[:, 1, :]))
            step(nc_.tensor_tensor_scan(te, til, til, 0.0, ALU.add, ALU.bypass))
            step(nc_.tensor_tensor(ts, te, til, ALU.subtract))
            step(nc_.scalar_tensor_tensor(out=off, in0=ts, scalar=float(P), in1=pre, op0=ALU.mult,
                                          op1=ALU.add))
            step(nc_.tensor_tensor(off, off, prev, ALU.subtract))
            step(nc_.tensor_scalar(off, off, -1.0, None, ALU.add))
            step(nc_.memset(pos, 0.0))
            for b in range(NK):
                step(nc_.scalar_tensor_tensor(out=tmp, in0=cum[:, b, :], scalar=off[:, b:b + 1],
                                              in1=eq[:, b, :], op0=ALU.add, op1=ALU.mult))
                step(nc_.tensor_tensor(pos, pos, tmp, ALU.add))
            step(nc_.tensor_copy(posi, pos))
            step(nc_.tensor_scalar(tmpi, posi, P - 1, None, ALU.bitwise_and))
            step(nc_.tensor_scalar(posi, posi, 7, None, ALU.arith_shift_right))
            step(nc_.scalar_tensor_tensor(out=pay[:, :, 4:5].rearrange("p t w -> p (t w)"), in0=tmpi,
                                          scalar=float(TW), in1=posi, op0=ALU.mult, op1=ALU.add))
            for h in range(2):
                nc_.tensor_copy(sring[:, h * HALF:(h + 1) * HALF, :],
                                pay[:, h * HALF:(h + 1) * HALF, :]).then_inc(s_sidx, 1)
            with dve.Fori(0, ET // U - 1) as i:
                for h in range(2):
                    for u in range(h * HALF, (h + 1) * HALF):
                        dve.wait_ge(s_scat[u], i * 16 + 16)
                    dve.nop(nofuse=True)
                    nc_.tensor_copy(sring[:, h * HALF:(h + 1) * HALF, :],
                                    pay[:, bass.ds(i * U + (U + h * HALF), HALF), :]).then_inc(s_sidx, 1)
            dve.wait_ge(s_pool, 8)
            step(nc_.memset(blk[:, :], 0.0))
            for b in range(NB - 1):
                step(nc_.scalar_tensor_tensor(out=blk[:, :], in0=rowf[:, :], scalar=te[:, b:b + 1],
                                              in1=blk[:, :], op0=ALU.is_ge, op1=ALU.add))
            step(nc_.tensor_copy(blki[:, :], blk[:, :]), "blocks")
            dve.wait_ge(s_srt, 16)
            step(nc_.tensor_copy(rowf[:, :], srt[:, :, 2]))

            def put_idx(word, lo, h):
                nc_.tensor_copy(idx[:, h * HALF:(h + 1) * HALF],
                                srt[:, bass.ds(lo, HALF), word]).then_inc(s_idx, 1)

            for l in range(L):
                if l == 0:
                    for b in range(0, NB, 4):
                        n = min(4, NB - b)
                        dve.wait_ge(s_t, 2 + b // 4 + 1)
                        ins = nc_.tensor_copy(hT[:, b * P:(b + n) * P], ps[:, b // 4, 0:n * P])
                else:
                    dve.wait_ge(s_used, U + NT * l)
                    for c in range(7):
                        n = min(512, NP - 512 * c)
                        ins = nc_.tensor_scalar(hT[:, 512 * c:512 * c + n], ps[:, c, 0:n], 0.0, None, ALU.max)
                step(ins, f"features{l}")
                if l == 0:
                    dve.wait_ge(s_const, 96)
                def take_x(i, first):
                    for u in range(XU):
                        if not first:
                            reg_wait(dve, s_xd[u], i * 16 + 16 * (NB // XU) * l)
                        for c in range(XC):
                            dve.wait_ge(s_xm, i * (XU * XC) + (XU * XC + NB * XC * l + u * XC + c + 1))
                            nc_.tensor_tensor(xst[:, u, c * G3:(c + 1) * G3], ps[:, (u * XC + c) % XB, 0:G3],
                                              bias[:, l * RF + c * G3:l * RF + (c + 1) * G3],
                                              ALU.add).then_inc(s_xe, 1)

                if l:
                    for u in range(XU):
                        dve.wait_ge(s_xd[u], 16 * (NB // XU) * l)
                take_x(0, True)
                with dve.Fori(1, NB // XU) as i:
                    take_x(i, False)
                put_idx(0, 0, 0)
                put_idx(0, HALF, 1)
                with dve.Fori(0, NT // U) as i:
                    for u in range(U):
                        dve.wait_ge(s_used, i * U + (NT * l + u + 1))
                        nc_.tensor_scalar(oh[:, u, :], iota_r[:, :], rowf[:, bass.ds(i * U + u, 1)], None,
                                          ALU.is_equal).then_inc(s_oh, 1)
                        if u % HALF == HALF - 1:
                            reg_wait(dve, s_used, i * U + (U + NT * l + u + 1))
                            put_idx(0, i * U + (U - HALF + u + 1), u // HALF)

            dve.wait_ge(s_used, U + NT * L)
            for c in range(7):
                n = min(512, NP - 512 * c)
                ins = nc_.tensor_copy(hT[:, 512 * c:512 * c + n], ps[:, c, 0:n])
            step(ins, "sums")

            def layer_norm(z, y):
                for b in range(NB):
                    ins = nc_.bn_stats(stats[:, b, :], z[:, b, :])
                step(ins)
                for b in range(NB):
                    ins = nc_.bn_aggr(mv[:, b, :], stats[:, b, :])
                step(ins)
                step(nc_.tensor_scalar(mv[:, :, 1], mv[:, :, 1], EPS, None, ALU.add), f"var{len(roots)}")
                roots.append(0)
                dve.wait_ge(s_a, len(roots))
                step(nc_.reciprocal(mv[:, :, 1], mv[:, :, 1]))
                for b in range(NB):
                    ins = nc_.tensor_scalar(y(b), z[:, b, :], mv[:, b, 0:1], mv[:, b, 1:2],
                                            ALU.subtract, ALU.mult)
                step(ins)

            roots = []
            T0 = 2 + 7
            for b in range(0, NB, 4):
                n = min(4, NB - b)
                dve.wait_ge(s_t, T0 + b // 4 + 1)
                ins = nc_.tensor_tensor(nodes[:, b:b + n, :].rearrange("p b d -> p (b d)"),
                                        nodes[:, b:b + n, :].rearrange("p b d -> p (b d)"),
                                        ps[:, b // 4, 0:n * P], ALU.add)
            step(ins)
            layer_norm(nodes, lambda b: rows[:, b, D:2 * D])
            step(nc_.memset(rows[:, :, 2 * D:HL], 1.0))
            ss, rt = sm[:, 9, 0:NB], sm[:, 10, 0:NB]
            for b in range(NB):
                step(nc_.tensor_tensor_reduce(out=sq, in0=rows[:, b, D:2 * D], in1=rows[:, b, D:2 * D],
                                              scale=1.0, scalar=0.0, op0=ALU.mult, op1=ALU.add,
                                              accum_out=ss[:, b:b + 1]))
            marks["squares"] = steps[0]
            dve.wait_ge(s_a, 2)
            step(nc_.reciprocal(rt, rt))
            for b in range(NB):
                ins = nc_.tensor_scalar(rows[:, b, 0:D], rows[:, b, D:2 * D], rt[:, b:b + 1], None, ALU.mult)
            step(ins, "rows")
            step(nc_.tensor_tensor(nm[:, :], ss, rt, ALU.mult))
            step(nc_.tensor_tensor(nm[:, :], nm[:, :], rt, ALU.mult))
            step(nc_.tensor_scalar(nm[:, :], nm[:, :], betab[:, 0:1], -1.0, ALU.mult, ALU.mult))
            step(nc_.tensor_copy(acc, rows[:, :, D:2 * D + 1]))
            for b in range(0, NB, 4):
                n = min(4, NB - b)
                dve.wait_ge(s_t, T0 + 7 + b // 4 + 1)
                ins = nc_.tensor_scalar(hT[:, b * P:(b + n) * P], ps[:, b // 4, 0:n * P], betab[:, 0:1],
                                        None, ALU.mult)
            step(ins, "turned")
            put_idx(1, 0, 0)
            put_idx(1, HALF, 1)

            def attend_step(k, j, on):
                if 0 in on:
                    s = j % 2
                    b = dve.value_load(blki[0:1, bass.ds(k, 1)], min_val=0, max_val=NB - 1)
                    if k is not j or j >= 2:
                        reg_wait(dve, s_sc, k - 1)
                    nc_.tensor_scalar(neg[:, s, :], iota_r[:, :], rowf[:, bass.ds(k, 1)], -BIG,
                                      ALU.not_equal, ALU.mult).then_inc(s_ny, 1)
                    nc_.tensor_copy(yb[:, s, :], hT[:, bass.ds(b * P, P)]).then_inc(s_ny, 1)
                if 1 in on:
                    s = (j - 1) % 2
                    v = k - 1
                    b = dve.value_load(blki[0:1, bass.ds(v, 1)], min_val=0, max_val=NB - 1)
                    dve.wait_ge(s_sc, v + 1)
                    nc_.tensor_reduce(tmx[:, s:s + 1], ps[:, 2 + s, 0:P], AX.X, ALU.max).then_inc(s_mx, 1)
                    if k is not j or j >= 3:
                        reg_wait(dve, s_ex, v * 2 - 2)
                    if k is not j or j >= 2:
                        reg_wait(dve, s_up, v)
                    nc_.tensor_copy(nold[:, s:s + 1], nm[:, bass.ds(b, 1)]).then_inc(s_no, 1)
                    dve.wait_ge(s_mx, v + 1)
                    nc_.scalar_tensor_tensor(out=nmn[:, s:s + 1], in0=tmx[:, s:s + 1], scalar=-1.0,
                                             in1=nm[:, bass.ds(b, 1)], op0=ALU.mult,
                                             op1=ALU.min).then_inc(s_nm, 1)
                    reg_wait(dve, s_nm, v + 1)
                    nc_.tensor_copy(nm[:, bass.ds(b, 1)], nmn[:, s:s + 1]).then_inc(s_up, 1)
                if 3 in on:
                    s = (j - 3) % 2
                    v = k - 3
                    b = dve.value_load(blki[0:1, bass.ds(v, 1)], min_val=0, max_val=NB - 1)
                    dve.wait_ge(s_pv, v + (U + 1))
                    if k is not j or j >= 4:
                        reg_wait(dve, s_ac, v)
                    a = acc.rearrange("p b w -> p (b w)")[:, bass.ds(b * (D + 1), D + 1)]
                    nc_.scalar_tensor_tensor(out=a, in0=a, scalar=scl[:, (j - 3) % 4:(j - 3) % 4 + 1],
                                             in1=ps[:, 6 + s, 0:D + 1],
                                             op0=ALU.mult, op1=ALU.add).then_inc(s_ac, 1)
                if 0 in on and j % HALF == HALF - 1:
                    h = j // HALF
                    reg_wait(dve, s_tr, k + 1)
                    put_idx(1, k + (U - HALF + 1), h)

            for k in range(U):
                attend_step(k, k, [t for t in (0, 1, 3) if k >= t])
            with dve.Fori(1, NT // U) as i:
                for j in range(U):
                    attend_step(i * U + j, j, [0, 1, 3])
            for k in range(NT, NT + 3):
                attend_step(k, k % U + U, [t for t in (1, 3) if k - t < NT])

            dve.wait_ge(s_ac, NT)
            den = sm[:, 11, 0:NB]
            step(nc_.reciprocal(den, acc[:, :, D]))
            for b in range(NB):
                ins = nc_.scalar_tensor_tensor(out=fin[:, b, :], in0=acc[:, b, 0:D], scalar=den[:, b:b + 1],
                                               in1=rows[:, b, D:2 * D], op0=ALU.mult, op1=ALU.add)
            step(ins)
            roots.append(0)
            layer_norm(fin, lambda b: fin[:, b, :])
            marks["result"] = steps[0]

        @block.sync
        def _(sp):
            sp.wait_ge(s_d, marks["cleared"])
            for a, t in ((src, srci), (dst, dsti), (edge_type, typei)):
                sp.dma_start(t[0:FULL, :], a[0:FULL * ET].rearrange("(p t) -> p t", t=ET)).then_inc(s_edges, 16)
                sp.dma_start(t[FULL:P, 0:REST], a[FULL * ET:E].rearrange("(p t) -> p t", p=1)).then_inc(s_edges, 16)
            sp.dma_start(nodes[:, 0:NB - 1, :],
                         x[0:(NB - 1) * P, :].rearrange("(b p) d -> p b d", p=P)).then_inc(s_const, 16)
            sp.dma_start(nodes[0:LAST, NB - 1, :], x[(NB - 1) * P:N, :]).then_inc(s_const, 16)
            sp.dma_start(nodes[LAST:P, NB - 1, :], x[0:P - LAST, :]).then_inc(s_const, 16)
            sp.dma_start(wsb[:, :, :], weights.rearrange("l r e f -> e (l r) f")).then_inc(s_const, 16)
            sp.dma_start(bias[:, :], biases.rearrange("l r f -> (l r f)").partition_broadcast(P)).then_inc(s_const, 16)
            sp.dma_start(betab[:, :], beta.partition_broadcast(P)).then_inc(s_const, 16)
            sp.wait_ge(s_d, marks["filler"])
            sp.dma_start(table.rearrange("(p t) w -> p (t w)", p=P),
                         srt[:, :, :].rearrange("p t w -> p (t w)")).then_inc(s_fill, 16)
            for u in range(U):
                sp.wait_ge(s_scat[u], 16 * (ET // U))
            sp.dma_start(srt[:, :, :].rearrange("p t w -> p (t w)"),
                         table.rearrange("(p t) w -> p (t w)", p=P)).then_inc(s_srt, 16)
            xv = xt.rearrange("(r n) d -> n r d", r=R)
            for l in range(L):
                with sp.Fori(0, NB // XU) as i:
                    for u in range(XU):
                        sp.wait_ge(s_xe, i * (XU * XC) + (XB + NB * XC * l + (u + 1) * XC))
                        sp.dma_start(xv[bass.ds(i * (XU * P) + u * P, P), :, :],
                                     xst[:, u, :].rearrange("p (r d) -> p r d", r=R)).then_inc(s_xd[u], 16)
            sp.wait_ge(s_d, marks["rows"])
            sp.dma_start(yt.rearrange("(b p) w -> p b w", p=P), rows).then_inc(s_yt, 16)
            sp.wait_ge(s_d, marks["result"])
            sp.dma_start(out[0:(NB - 1) * P, :].rearrange("(b p) d -> p b d", p=P),
                         fin[:, 0:NB - 1, :]).then_inc(s_out, 16)
            sp.dma_start(out[(NB - 1) * P:N, :], fin[0:LAST, NB - 1, :]).then_inc(s_out, 16)
            sp.wait_ge(s_out, 32)

        @block.gpsimd
        def _(pool):
            nc_ = pool
            nc_.memset(ident[:, :], 0.0).then_inc(s_pool, 1)
            nc_.memset(ltri, 1.0).then_inc(s_pool, 1)
            nc_.memset(ones, 1.0).then_inc(s_pool, 1)
            nc_.iota(iota_r[:, :], pattern=[[1, P]], base=0, channel_multiplier=0,
                     allow_small_or_imprecise_dtypes=True).then_inc(s_pool, 1)
            nc_.iota(rowf[:, :], pattern=[[1, TW]], base=0, channel_multiplier=0,
                     allow_small_or_imprecise_dtypes=True).then_inc(s_pool, 1)
            pool.wait_ge(s_pool, 5)
            nc_.affine_select(out=ident[:, :], in_=ident[:, :], compare_op=ALU.not_equal, fill=1.0, base=0,
                              pattern=[[-1, P]], channel_multiplier=1).then_inc(s_pool, 1)
            nc_.affine_select(out=ltri, in_=ltri, compare_op=ALU.is_gt, fill=0.0, base=0,
                              pattern=[[1, P]], channel_multiplier=-1).then_inc(s_pool, 1)
            pool.wait_ge(s_pool, 7)
            nc_.tensor_copy(identb[:, :], ident[:, :]).then_inc(s_pool, 1)
            pool.wait_ge(s_fill, 16)
            with pool.Fori(0, ET // U) as i:
                for u in range(U):
                    if u % HALF == 0:
                        reg_wait(pool, s_sidx, i * 2 + (u // HALF + 1))
                    pool.indirect_dma_start(
                        out=table, out_offset=bass.IndirectOffsetOnAxis(ap=sring[:, u, 4:5], axis=0),
                        in_=sring[:, u, 0:PAYS], in_offset=None).then_inc(s_scat[u], 16)

            def gathers(source, to, base, used, lag):
                n = base * NT
                with pool.Fori(0, NT // U) as i:
                    for u in range(U):
                        if u % HALF == 0:
                            reg_wait(pool, s_idx, i * 2 + (base * (NT // HALF + 2) + u // HALF + 1))
                        reg_wait(pool, used, i * U + (lag + u + 1))
                        pool.indirect_dma_start(
                            out=to[:, u, :], out_offset=None, in_=source,
                            in_offset=bass.IndirectOffsetOnAxis(ap=idx[:, u:u + 1], axis=0),
                        ).then_inc(s_g[u], 16)

            for l in range(L):
                for u in range(XU):
                    pool.wait_ge(s_xd[u], 16 * (NB // XU) * (l + 1))
                gathers(xt, grow, l, s_used, NT * l)
            pool.wait_ge(s_yt, 16)
            gathers(yt, gat, L, s_pv, 0)

        @block.tensor
        def _(pe):
            pe.wait_ge(s_pool, 8)
            pe.wait_ge(s_d, marks["counts"])
            pe.matmul(ps[:, 0, 0:NK], ltri, sm[:, 1, :], start=True, stop=True).then_inc(s_t, 1)
            pe.matmul(ps[:, 1, 0:NK], ones, sm[:, 1, :], start=True, stop=True).then_inc(s_t, 1)

            def turn(source):
                for b in range(NB):
                    mm = pe.transpose(ps[:, b // 4, (b % 4) * P:(b % 4 + 1) * P], source(b), ident[:, :])
                    if b % 4 == 3 or b == NB - 1:
                        mm.then_inc(s_t, 1)

            pe.wait_ge(s_const, 96)
            pe.wait_ge(s_d, marks["totals"])
            turn(lambda b: nodes[:, b, :])
            for l in range(L):
                pe.wait_ge(s_d, marks[f"features{l}"])
                with pe.Fori(0, NB // XU) as i:
                    for u in range(XU):
                        pe.wait_ge(s_hb, i * XU + (NB * l + u + 1))
                        for c in range(XC):
                            q = u * XC + c
                            pe.wait_ge(s_xe, i * (XU * XC) + (NB * XC * l + q + 1))
                            pe.matmul(ps[:, q % XB, 0:G3], hblk[:, u, :],
                                      wsb[:, l * R + 3 * c:l * R + 3 * c + 3, :].rearrange("p r d -> p (r d)"),
                                      start=True, stop=True).then_inc(s_xm, 1)
                pe.wait_ge(s_xe, XB + NB * XC * (l + 1))
                for c in range(7):
                    pe.matmul(ps[:, c, :], zerob[:, 0:P], zerob[:, :], start=True, stop=False,
                              skip_group_check=True)
                with pe.Fori(0, NT // U) as i:
                    for u in range(U):
                        b = pe.value_load(blki[0:1, bass.ds(i * U + u, 1)], min_val=0, max_val=NB - 1)
                        pe.wait_ge(s_g[u], i * 16 + 16 * (NT // U * l + 1))
                        pe.wait_ge(s_oh, i * U + (NT * l + u + 1))
                        pe.matmul(agg[:, bass.ds(b * P, P)], grow[:, u, :], oh[:, u, :], start=False,
                                  stop=False, skip_group_check=True).then_inc(s_used, 1)
            pe.wait_ge(s_d, marks["sums"])
            turn(lambda b: hT[:, b * P:(b + 1) * P])
            pe.wait_ge(s_d, marks["rows"])
            turn(lambda b: rows[:, b, 0:D])
            pe.wait_ge(s_d, marks["turned"])

            def attend_step(k, j, on):
                later = k is not j
                if 0 in on:
                    pe.wait_ge(s_g[j], turn_count(k, j, later))
                    if later or j >= 2:
                        pe.wait_ge(s_gt, k - 1)
                    pe.transpose(ps[:, j % 2, 0:P], gat[:, j, 0:D], ident[:, :]).then_inc(s_tr, 1)
                if 1 in on:
                    v, s = k - 1, (j - 1) % 2
                    pe.wait_ge(s_gt, v + 1)
                    pe.wait_ge(s_ny, v * 2 + 2)
                    if later or j >= 3:
                        pe.wait_ge(s_ex, v * 2 - 2)
                    pe.matmul(ps[:, 2 + s, 0:P], yb[:, s, :], gt[:, s, :], start=True, stop=False)
                    pe.matmul(ps[:, 2 + s, 0:P], neg[:, s, :], identb[:, :], start=False,
                              stop=True).then_inc(s_sc, 1)
                if 2 in on:
                    v, s = k - 2, (j - 2) % 2
                    pe.wait_ge(s_ex, v * 2 + 1)
                    if later or j >= 4:
                        pe.wait_ge(s_pc, v - 1)
                    pe.transpose(ps[:, 4 + s, 0:P], pr[:, s, :], ident[:, :]).then_inc(s_pt, 1)
                if 3 in on:
                    v, s = k - 3, (j - 3) % 2
                    pe.wait_ge(s_pc, v + 1)
                    if later or j >= 5:
                        pe.wait_ge(s_ac, v - 1)
                    pe.matmul(ps[:, 6 + s, 0:D + 1], pt[:, s, :], gat[:, (j - 3) % U, D:2 * D + 1],
                              start=True, stop=True).then_inc(s_pv, 1)

            def turn_count(k, j, later):
                if later:
                    return (k - j) * (16 // U) + 16 * (NT // U * L + 1)
                return 16 * (NT // U * L + 1)

            for k in range(U):
                attend_step(k, k, [t for t in range(4) if k >= t])
            with pe.Fori(1, NT // U) as i:
                for j in range(U):
                    attend_step(i * U + j, j, [0, 1, 2, 3])
            for k in range(NT, NT + 3):
                attend_step(k, k % U + U, [t for t in range(1, 4) if k - t < NT])

        @block.scalar
        def _(act):
            for l in range(L):
                act.wait_ge(s_d, marks[f"features{l}"])
                with act.Fori(0, NB // XU) as i:
                    for u in range(XU):
                        reg_wait(act, s_xm, i * (XU * XC) + (NB * XC * l + (u + 1) * XC))
                        act.copy(hblk[:, u, :], hT[:, bass.ds(i * (XU * P) + u * P, P)]).then_inc(s_hb, 1)
            act.wait_ge(s_d, marks["var0"])
            act.activation(mv[:, :, 1], mv[:, :, 1], ACT.Sqrt).then_inc(s_a, 1)
            act.wait_ge(s_d, marks["squares"])
            act.activation(sm[:, 10, 0:NB], sm[:, 9, 0:NB], ACT.Sqrt).then_inc(s_a, 1)
            act.wait_ge(s_d, marks["turned"])

            def attend_step(k, j, on):
                later = k is not j
                if 0 in on:
                    s = j % 2
                    act.wait_ge(s_tr, k + 1)
                    if later or j >= 2:
                        act.wait_ge(s_sc, k - 1)
                    act.activation(gt[:, s, :], ps[:, s, 0:P], ACT.Copy).then_inc(s_gt, 1)
                if 1 in on:
                    v, s = k - 1, (j - 1) % 2
                    act.wait_ge(s_nm, v + 1)
                    if later or j >= 3:
                        act.wait_ge(s_pt, v - 1)
                    act.activation(pr[:, s, :], ps[:, 2 + s, 0:P], ACT.Exp,
                                   bias=nmn[:, s:s + 1]).then_inc(s_ex, 1)
                    act.wait_ge(s_no, v + 1)
                    if later or j >= 5:
                        act.wait_ge(s_ac, v - 3)
                    act.activation(scl[:, (j - 1) % 4:(j - 1) % 4 + 1], nold[:, s:s + 1], ACT.Exp,
                                   bias=nmn[:, s:s + 1], scale=-1.0).then_inc(s_ex, 1)
                if 2 in on:
                    v, s = k - 2, (j - 2) % 2
                    act.wait_ge(s_pt, v + 1)
                    if later or j >= 4:
                        act.wait_ge(s_pv, v + (U - 1))
                    act.activation(pt[:, s, :], ps[:, 4 + s, 0:P], ACT.Copy).then_inc(s_pc, 1)

            for k in range(U):
                attend_step(k, k, [t for t in range(3) if k >= t])
            with act.Fori(1, NT // U) as i:
                for j in range(U):
                    attend_step(i * U + j, j, [0, 1, 2])
            for k in range(NT, NT + 2):
                attend_step(k, k % U + U, [t for t in range(1, 3) if k - t < NT])
            act.wait_ge(s_d, marks["var2"])
            act.activation(mv[:, :, 1], mv[:, :, 1], ACT.Sqrt).then_inc(s_a, 1)


_INS = ['x', 'src', 'dst', 'edge_type_9', 'L0_gnn_weights', 'L0_gnn_biases', 'L1_gnn_beta']


def kernel(**inputs):
    import numpy as _np
    import concourse.bacc as _bacc
    from concourse import mybir as _mybir
    from concourse.bass_utils import run_bass_kernel_spmd as _run

    nc = _bacc.Bacc("TRN2", target_bir_lowering=False, num_devices=1)
    arrays, args = {}, []
    for name in _INS:
        a = _np.ascontiguousarray(inputs[name])
        arrays[f"in_{name}_dram"] = a
        args.append(nc.dram_tensor(f"in_{name}_dram", a.shape, _mybir.dt.from_np(a.dtype), kind="ExternalInput").ap())
    n, d = inputs['x'].shape
    args.append(nc.dram_tensor("out_0_dram", (n, d), _mybir.dt.float32, kind="ExternalOutput").ap())
    gnn_program(nc, *args)
    r = _run(nc, [arrays], core_ids=[0])
    return r.results[0]["out_0_dram"]
```

```python
from contextlib import ExitStack

import concourse.bass as bass
from concourse import mybir

F32 = mybir.dt.float32
BF16 = mybir.dt.bfloat16
I32 = mybir.dt.int32
I16 = mybir.dt.int16
ALU = mybir.AluOpType
ACT = mybir.ActivationFunctionType
AX = mybir.AxisListType

P = 128
U = 8
HALF = 4
G = 2
RING = 24
BIG = 1.0e30
EPS = 1e-05
NO_ROW = 999


def gnn_program(nc, x, src, dst, edge_type, weights, biases, beta, out):
    N, D = x.shape
    E = src.shape[0]
    L, R = weights.shape[0], weights.shape[1]
    NB = -(-N // P)
    NP = NB * P
    LAST = N - (NB - 1) * P
    RF = R * D
    ET = -(-E // (P * U)) * U
    FULL = E // ET
    REST = E - FULL * ET
    assert D == P and FULL == P - 1 and G == 2
    NK = NB + 1
    PAD_ROW = NB * P
    GP = G * P
    NT = -(-(E + NB * (GP - 1)) // GP * G // U) * U
    NG = NT // G
    TW = NT + RING
    SLACK = P * ET - E
    assert (E + NB * (GP - 1)) // GP * G <= NT and NT + G * -(-SLACK // GP) <= TW
    SG = RING // G
    LEAD = NG % SG
    assert LEAD > 5 and RING % HALF == 0 and LEAD * G % HALF == 0
    PAYS = 4
    HL = 2 * D + 4
    G3 = 3 * D
    XC = RF // G3
    XB = 5
    XU = 5
    assert NB % XU == 0 and RF % G3 == 0

    table = nc.dram_tensor("sorted_edges", (P * TW, PAYS), I32, kind="Internal").ap()
    xt = nc.dram_tensor("x_of_type", (R * NP, D), F32, kind="Internal").ap()
    yt = nc.dram_tensor("attended_rows", (NP, HL), F32, kind="Internal").ap()

    with ExitStack() as ctx:
        def sb(name, shape, dt=F32):
            return ctx.enter_context(nc.sbuf_tensor(name, shape, dt))

        def sem(name):
            return ctx.enter_context(nc.semaphore(name))

        nodes = sb("nodes", [P, NB, D])
        wsb = sb("wsb", [P, L * R, D])
        bias = sb("bias", [P, L * RF])
        hT = sb("hT", [P, NP])
        ident = sb("ident", [P, P])
        identb = sb("identb", [P, P], BF16)
        zerob = sb("zerob", [P, 512], BF16)
        iota_r = sb("iota_r", [P, P])
        srt = sb("srt", [P, TW, PAYS], I32)
        rowf = sb("rowf", [P, TW])
        blk = sb("blk", [P, TW])
        blki = sb("blki", [P, TW], I32)
        betab = sb("betab", [P, 1])
        idx = sb("idx", [P, RING], I32)
        oh = sb("oh", [P, U, P])
        sm = sb("sm", [P, 12, NK])
        smi = sb("smi", [P, 2, NK], I32)

        REGION = 27 * 1024
        region = sb("region", [P, REGION])
        used = [0]

        def part(words, dt=F32):
            a = region[:, used[0]:used[0] + words]
            used[0] += words
            assert used[0] <= REGION, used[0]
            return a if dt == F32 else a.bitcast(dt)

        eq = part(NK * ET // 2, BF16).rearrange("p (b t) -> p b t", b=NK)
        cum = part(NK * ET // 2, I16).rearrange("p (b t) -> p b t", b=NK)
        pay = part(ET * (PAYS + 1), I32).rearrange("p (t w) -> p t w", w=PAYS + 1)
        sring = part(U * (PAYS + 1), I32).rearrange("p (t w) -> p t w", w=PAYS + 1)
        keyb = part(ET // 2, BF16)
        pos = part(ET)
        posi = part(ET, I32)
        tmp, tmpi = blk[:, 0:ET], blki[:, 0:ET]
        srci, dsti, typei = (hT[:, n * ET:(n + 1) * ET].bitcast(I32) for n in range(3))
        used[0] = 0
        grow = part(U * D).rearrange("p (u d) -> p u d", u=U)
        hblk = part(XU * P).rearrange("p (u d) -> p u d", u=XU)
        xst = part(XU * RF).rearrange("p (u w) -> p u w", u=XU)
        used[0] = 0
        gat = part(RING * HL).rearrange("p (u w) -> p u w", u=RING)
        rows = part(NB * HL).rearrange("p (b w) -> p b w", b=NB)
        acc = part(NB * (D + 1)).rearrange("p (b w) -> p b w", b=NB)
        gt = part(2 * GP).rearrange("p (s w) -> p s w", s=2)
        yb = part(2 * P).rearrange("p (s w) -> p s w", s=2)
        neg = part(GP, BF16).rearrange("p (s w) -> p s w", s=2)
        pr = part(2 * GP).rearrange("p (s w) -> p s w", s=2)
        pt = part(2 * GP).rearrange("p (s w) -> p s w", s=2)
        nmn = part(4)
        nold = part(4)
        scl = part(4)
        tmx = part(4)
        fin = part(NB * D).rearrange("p (b w) -> p b w", b=NB)
        sq = part(D)
        ltri, ones = oh[:, 0, :], oh[:, 1, :]

        stats = sb("stats", [P, NB, 6])
        mv = sb("mv", [P, NB, 2])
        nm = sb("nm", [P, NB])

        ps = ctx.enter_context(nc.psum_tensor("ps", [P, 8, 512], F32))
        agg = ps[:, 0:7, :].rearrange("p k n -> p (k n)")

        s_edges = sem("s_edges")
        s_const = sem("s_const")
        s_pool = sem("s_pool")
        s_d = sem("s_d")
        s_a = sem("s_a")
        s_t = sem("s_t")
        s_fill = sem("s_fill")
        s_sidx = sem("s_sidx")
        s_scat = [sem(f"s_scat{u}") for u in range(U)]
        s_srt = sem("s_srt")
        s_hb = sem("s_hb")
        s_xm = sem("s_xm")
        s_xe = sem("s_xe")
        s_xd = [sem(f"s_xd{u}") for u in range(XU)]
        s_idx = sem("s_idx")
        s_g = [sem(f"s_g{u}") for u in range(RING)]
        s_oh = sem("s_oh")
        s_used = sem("s_used")
        s_yt = sem("s_yt")
        s_tr = sem("s_tr")
        s_gt = sem("s_gt")
        s_ny = sem("s_ny")
        s_sc = sem("s_sc")
        s_mx = sem("s_mx")
        s_nm = sem("s_nm")
        s_no = sem("s_no")
        s_up = sem("s_up")
        s_ex = sem("s_ex")
        s_pt = sem("s_pt")
        s_pc = sem("s_pc")
        s_pv = sem("s_pv")
        s_ac = sem("s_ac")
        s_out = sem("s_out")

        marks = {}

        block = ctx.enter_context(nc.Block())

        def reg_wait(eng, s, value):
            eng.wait_ge(s, value)
            eng.nop(nofuse=True)

        @block.vector
        def _(dve):
            steps = [0]

            def step(ins, mark=None):
                steps[0] += 1
                ins.then_inc(s_d, 1)
                dve.wait_ge(s_d, steps[0])
                if mark:
                    marks[mark] = steps[0]

            dve.sem_inc(s_used, U)
            dve.sem_inc(s_pv, SG)
            dve.sem_inc(s_xe, XB)
            dve.sem_inc(s_xm, XU * XC)
            nc_ = dve
            step(nc_.memset(srci, PAD_ROW))
            step(nc_.memset(dsti, 0))
            step(nc_.memset(typei, 0), "cleared")
            nc_.memset(zerob[:, :], 0.0)
            step(nc_.memset(srt[:, :, :], 0))
            step(nc_.memset(srt[:, :, 2:3], NO_ROW), "filler")

            dve.wait_ge(s_edges, 96)
            step(nc_.tensor_scalar(tmpi, srci, 7, None, ALU.arith_shift_right))
            step(nc_.tensor_copy(keyb, tmpi))
            step(nc_.tensor_scalar(posi, tmpi, float(NB - 1), -float(P), ALU.min, ALU.mult))
            step(nc_.tensor_tensor(pay[:, :, 2:3].rearrange("p t w -> p (t w)"), srci, posi, ALU.add))
            step(nc_.tensor_copy(pay[:, :, 1:2].rearrange("p t w -> p (t w)"), dsti))
            step(nc_.memset(pay[:, :, 3:4], 0))
            step(nc_.scalar_tensor_tensor(out=pay[:, :, 0:1].rearrange("p t w -> p (t w)"), in0=typei,
                                          scalar=float(NP), in1=dsti, op0=ALU.mult, op1=ALU.add))
            for b in range(NK):
                ins = nc_.tensor_scalar(eq[:, b, :], keyb, float(b), None, ALU.is_equal)
            step(ins)
            eqf = eq.rearrange("p b t -> p (b t)")
            step(nc_.tensor_tensor_scan(cum.rearrange("p b t -> p (b t)"), eqf, eqf, 0.0,
                                        ALU.add, ALU.bypass))
            ends, cnt, prev, pre, tot, til, te, ts, off = (sm[:, i, :] for i in range(9))
            step(nc_.tensor_copy(ends, cum[:, :, ET - 1]))
            step(nc_.memset(prev[:, 0:1], 0.0))
            step(nc_.tensor_copy(prev[:, 1:NK], ends[:, 0:NK - 1]))
            step(nc_.tensor_tensor(cnt, ends, prev, ALU.subtract), "counts")
            dve.wait_ge(s_t, 2)
            step(nc_.tensor_copy(pre, ps[:, 0, 0:NK]))
            step(nc_.tensor_copy(tot, ps[:, 1, 0:NK]), "totals")
            step(nc_.tensor_scalar(tot, tot, float(GP - 1), None, ALU.add))
            step(nc_.tensor_copy(smi[:, 0, :], tot))
            step(nc_.tensor_scalar(smi[:, 1, :], smi[:, 0, :], 8, None, ALU.arith_shift_right))
            step(nc_.tensor_scalar(til, smi[:, 1, :], float(G), None, ALU.mult))
            step(nc_.tensor_tensor_scan(te, til, til, 0.0, ALU.add, ALU.bypass))
            step(nc_.tensor_tensor(ts, te, til, ALU.subtract))
            step(nc_.scalar_tensor_tensor(out=off, in0=ts, scalar=float(P), in1=pre, op0=ALU.mult,
                                          op1=ALU.add))
            step(nc_.tensor_tensor(off, off, prev, ALU.subtract))
            step(nc_.tensor_scalar(off, off, -1.0, None, ALU.add))
            step(nc_.memset(pos, 0.0))
            for b in range(NK):
                step(nc_.scalar_tensor_tensor(out=tmp, in0=cum[:, b, :], scalar=off[:, b:b + 1],
                                              in1=eq[:, b, :], op0=ALU.add, op1=ALU.mult))
                step(nc_.tensor_tensor(pos, pos, tmp, ALU.add))
            step(nc_.tensor_copy(posi, pos))
            step(nc_.tensor_scalar(tmpi, posi, P - 1, None, ALU.bitwise_and))
            step(nc_.tensor_scalar(posi, posi, 7, None, ALU.arith_shift_right))
            step(nc_.scalar_tensor_tensor(out=pay[:, :, 4:5].rearrange("p t w -> p (t w)"), in0=tmpi,
                                          scalar=float(TW), in1=posi, op0=ALU.mult, op1=ALU.add))
            for h in range(2):
                nc_.tensor_copy(sring[:, h * HALF:(h + 1) * HALF, :],
                                pay[:, h * HALF:(h + 1) * HALF, :]).then_inc(s_sidx, 1)
            with dve.Fori(0, ET // U - 1) as i:
                for h in range(2):
                    for u in range(h * HALF, (h + 1) * HALF):
                        dve.wait_ge(s_scat[u], i * 16 + 16)
                    dve.nop(nofuse=True)
                    nc_.tensor_copy(sring[:, h * HALF:(h + 1) * HALF, :],
                                    pay[:, bass.ds(i * U + (U + h * HALF), HALF), :]).then_inc(s_sidx, 1)
            dve.wait_ge(s_pool, 8)
            step(nc_.memset(blk[:, :], 0.0))
            for b in range(NB - 1):
                step(nc_.scalar_tensor_tensor(out=blk[:, :], in0=rowf[:, :], scalar=te[:, b:b + 1],
                                              in1=blk[:, :], op0=ALU.is_ge, op1=ALU.add))
            step(nc_.tensor_copy(blki[:, :], blk[:, :]), "blocks")
            dve.wait_ge(s_srt, 16)
            step(nc_.tensor_copy(rowf[:, :], srt[:, :, 2]))

            def put_idx(word, lo, h):
                nc_.tensor_copy(idx[:, h * HALF:(h + 1) * HALF],
                                srt[:, bass.ds(lo, HALF), word]).then_inc(s_idx, 1)

            for l in range(L):
                if l == 0:
                    for b in range(0, NB, 4):
                        n = min(4, NB - b)
                        dve.wait_ge(s_t, 2 + b // 4 + 1)
                        ins = nc_.tensor_copy(hT[:, b * P:(b + n) * P], ps[:, b // 4, 0:n * P])
                else:
                    dve.wait_ge(s_used, U + NT * l)
                    for c in range(7):
                        n = min(512, NP - 512 * c)
                        ins = nc_.tensor_scalar(hT[:, 512 * c:512 * c + n], ps[:, c, 0:n], 0.0, None, ALU.max)
                step(ins, f"features{l}")
                if l == 0:
                    dve.wait_ge(s_const, 96)
                def take_x(i, first):
                    for u in range(XU):
                        if not first:
                            reg_wait(dve, s_xd[u], i * 16 + 16 * (NB // XU) * l)
                        for c in range(XC):
                            dve.wait_ge(s_xm, i * (XU * XC) + (XU * XC + NB * XC * l + u * XC + c + 1))
                            nc_.tensor_tensor(xst[:, u, c * G3:(c + 1) * G3], ps[:, (u * XC + c) % XB, 0:G3],
                                              bias[:, l * RF + c * G3:l * RF + (c + 1) * G3],
                                              ALU.add).then_inc(s_xe, 1)

                if l:
                    for u in range(XU):
                        dve.wait_ge(s_xd[u], 16 * (NB // XU) * l)
                take_x(0, True)
                with dve.Fori(1, NB // XU) as i:
                    take_x(i, False)
                put_idx(0, 0, 0)
                put_idx(0, HALF, 1)
                with dve.Fori(0, NT // U) as i:
                    for u in range(U):
                        dve.wait_ge(s_used, i * U + (NT * l + u + 1))
                        nc_.tensor_scalar(oh[:, u, :], iota_r[:, :], rowf[:, bass.ds(i * U + u, 1)], None,
                                          ALU.is_equal).then_inc(s_oh, 1)
                        if u % HALF == HALF - 1:
                            reg_wait(dve, s_used, i * U + (U + NT * l + u + 1))
                            put_idx(0, i * U + (U - HALF + u + 1), u // HALF)

            dve.wait_ge(s_used, U + NT * L)
            for c in range(7):
                n = min(512, NP - 512 * c)
                ins = nc_.tensor_copy(hT[:, 512 * c:512 * c + n], ps[:, c, 0:n])
            step(ins, "sums")

            def layer_norm(z, y):
                for b in range(NB):
                    ins = nc_.bn_stats(stats[:, b, :], z[:, b, :])
                step(ins)
                for b in range(NB):
                    ins = nc_.bn_aggr(mv[:, b, :], stats[:, b, :])
                step(ins)
                step(nc_.tensor_scalar(mv[:, :, 1], mv[:, :, 1], EPS, None, ALU.add), f"var{len(roots)}")
                roots.append(0)
                dve.wait_ge(s_a, len(roots))
                step(nc_.reciprocal(mv[:, :, 1], mv[:, :, 1]))
                for b in range(NB):
                    ins = nc_.tensor_scalar(y(b), z[:, b, :], mv[:, b, 0:1], mv[:, b, 1:2],
                                            ALU.subtract, ALU.mult)
                step(ins)

            roots = []
            T0 = 2 + 7
            for b in range(0, NB, 4):
                n = min(4, NB - b)
                dve.wait_ge(s_t, T0 + b // 4 + 1)
                ins = nc_.tensor_tensor(nodes[:, b:b + n, :].rearrange("p b d -> p (b d)"),
                                        nodes[:, b:b + n, :].rearrange("p b d -> p (b d)"),
                                        ps[:, b // 4, 0:n * P], ALU.add)
            step(ins)
            layer_norm(nodes, lambda b: rows[:, b, D:2 * D])
            step(nc_.memset(rows[:, :, 2 * D:HL], 1.0))
            ss, rt = sm[:, 9, 0:NB], sm[:, 10, 0:NB]
            for b in range(NB):
                step(nc_.tensor_tensor_reduce(out=sq, in0=rows[:, b, D:2 * D], in1=rows[:, b, D:2 * D],
                                              scale=1.0, scalar=0.0, op0=ALU.mult, op1=ALU.add,
                                              accum_out=ss[:, b:b + 1]))
            marks["squares"] = steps[0]
            dve.wait_ge(s_a, 2)
            step(nc_.reciprocal(rt, rt))
            for b in range(NB):
                ins = nc_.tensor_scalar(rows[:, b, 0:D], rows[:, b, D:2 * D], rt[:, b:b + 1], None, ALU.mult)
            step(ins, "rows")
            step(nc_.tensor_tensor(nm[:, :], ss, rt, ALU.mult))
            step(nc_.tensor_tensor(nm[:, :], nm[:, :], rt, ALU.mult))
            step(nc_.tensor_scalar(nm[:, :], nm[:, :], betab[:, 0:1], -1.0, ALU.mult, ALU.mult))
            step(nc_.tensor_copy(acc, rows[:, :, D:2 * D + 1]))
            for b in range(0, NB, 4):
                n = min(4, NB - b)
                dve.wait_ge(s_t, T0 + 7 + b // 4 + 1)
                ins = nc_.tensor_scalar(hT[:, b * P:(b + n) * P], ps[:, b // 4, 0:n * P], betab[:, 0:1],
                                        None, ALU.mult)
            step(ins, "turned")
            for q in range(4):
                put_idx(1, q * HALF, q)

            def attend_step(k, j, on):
                later = k is not j
                if 0 in on:
                    s = j % 2
                    b = dve.value_load(blki[0:1, bass.ds(k * G, 1)], min_val=0, max_val=NB - 1)
                    if later or j >= 2:
                        reg_wait(dve, s_sc, k - 1)
                    for t in range(G):
                        nc_.tensor_scalar(neg[:, s, t * P:(t + 1) * P], iota_r[:, :],
                                          rowf[:, bass.ds(k * G + t, 1)], -BIG,
                                          ALU.not_equal, ALU.mult).then_inc(s_ny, 1)
                    nc_.tensor_copy(yb[:, s, :], hT[:, bass.ds(b * P, P)]).then_inc(s_ny, 1)
                if 1 in on:
                    s = (j - 1) % 2
                    v = k - 1
                    b = dve.value_load(blki[0:1, bass.ds(v * G, 1)], min_val=0, max_val=NB - 1)
                    if later or j >= 3:
                        dve.wait_ge(s_ex, v * 2 - 2)
                    if later or j >= 2:
                        reg_wait(dve, s_up, v)
                    nc_.tensor_copy(nold[:, s:s + 1], nm[:, bass.ds(b, 1)]).then_inc(s_no, 1)
                    dve.wait_ge(s_sc, v + 1)
                    nc_.tensor_reduce(tmx[:, s:s + 1], ps[:, 2 + s, 0:GP], AX.X, ALU.max).then_inc(s_mx, 1)
                    dve.wait_ge(s_no, v + 1)
                    dve.wait_ge(s_mx, v + 1)
                    nc_.scalar_tensor_tensor(out=nmn[:, s:s + 1], in0=tmx[:, s:s + 1], scalar=-1.0,
                                             in1=nold[:, s:s + 1], op0=ALU.mult,
                                             op1=ALU.min).then_inc(s_nm, 1)
                    reg_wait(dve, s_nm, v + 1)
                    nc_.tensor_copy(nm[:, bass.ds(b, 1)], nmn[:, s:s + 1]).then_inc(s_up, 1)
                if 5 in on:
                    v = k - 5
                    b = dve.value_load(blki[0:1, bass.ds(v * G, 1)], min_val=0, max_val=NB - 1)
                    dve.wait_ge(s_pv, v + (SG + 1))
                    if later or j >= 6:
                        reg_wait(dve, s_ac, v)
                    a = acc.rearrange("p b w -> p (b w)")[:, bass.ds(b * (D + 1), D + 1)]
                    nc_.scalar_tensor_tensor(out=a, in0=a, scalar=scl[:, (j - 5) % 4:(j - 5) % 4 + 1],
                                             in1=ps[:, 6 + (j - 5) % 2, 0:D + 1],
                                             op0=ALU.mult, op1=ALU.add).then_inc(s_ac, 1)
                if 0 in on and j % 2 == 1:
                    q = j // 2 + 4
                    if later or q * HALF >= RING:
                        reg_wait(dve, s_tr, k + (2 * (4 - RING // HALF) + 1))
                    put_idx(1, k * G + (4 * HALF - G), q % (RING // HALF))

            for k in range(LEAD):
                attend_step(k, k, [t for t in (0, 1, 5) if k >= t])
            with dve.Fori(0, NG // SG) as i:
                for j in range(LEAD, LEAD + SG):
                    attend_step(i * SG + j, j, [0, 1, 5])
            for k in range(NG, NG + 5):
                attend_step(k, k - NG + LEAD + 2 * SG, [t for t in (1, 5) if k - t < NG])

            dve.wait_ge(s_ac, NG)
            den = sm[:, 11, 0:NB]
            step(nc_.reciprocal(den, acc[:, :, D]))
            for b in range(NB):
                ins = nc_.scalar_tensor_tensor(out=fin[:, b, :], in0=acc[:, b, 0:D], scalar=den[:, b:b + 1],
                                               in1=rows[:, b, D:2 * D], op0=ALU.mult, op1=ALU.add)
            step(ins)
            roots.append(0)
            layer_norm(fin, lambda b: fin[:, b, :])
            marks["result"] = steps[0]

        @block.sync
        def _(sp):
            sp.wait_ge(s_d, marks["cleared"])
            for a, t in ((src, srci), (dst, dsti), (edge_type, typei)):
                sp.dma_start(t[0:FULL, :], a[0:FULL * ET].rearrange("(p t) -> p t", t=ET)).then_inc(s_edges, 16)
                sp.dma_start(t[FULL:P, 0:REST], a[FULL * ET:E].rearrange("(p t) -> p t", p=1)).then_inc(s_edges, 16)
            sp.dma_start(nodes[:, 0:NB - 1, :],
                         x[0:(NB - 1) * P, :].rearrange("(b p) d -> p b d", p=P)).then_inc(s_const, 16)
            sp.dma_start(nodes[0:LAST, NB - 1, :], x[(NB - 1) * P:N, :]).then_inc(s_const, 16)
            sp.dma_start(nodes[LAST:P, NB - 1, :], x[0:P - LAST, :]).then_inc(s_const, 16)
            sp.dma_start(wsb[:, :, :], weights.rearrange("l r e f -> e (l r) f")).then_inc(s_const, 16)
            sp.dma_start(bias[:, :], biases.rearrange("l r f -> (l r f)").partition_broadcast(P)).then_inc(s_const, 16)
            sp.dma_start(betab[:, :], beta.partition_broadcast(P)).then_inc(s_const, 16)
            sp.wait_ge(s_d, marks["filler"])
            sp.dma_start(table.rearrange("(p t) w -> p (t w)", p=P),
                         srt[:, :, :].rearrange("p t w -> p (t w)")).then_inc(s_fill, 16)
            for u in range(U):
                sp.wait_ge(s_scat[u], 16 * (ET // U))
            sp.dma_start(srt[:, :, :].rearrange("p t w -> p (t w)"),
                         table.rearrange("(p t) w -> p (t w)", p=P)).then_inc(s_srt, 16)
            xv = xt.rearrange("(r n) d -> n r d", r=R)
            for l in range(L):
                with sp.Fori(0, NB // XU) as i:
                    for u in range(XU):
                        sp.wait_ge(s_xe, i * (XU * XC) + (XB + NB * XC * l + (u + 1) * XC))
                        sp.dma_start(xv[bass.ds(i * (XU * P) + u * P, P), :, :],
                                     xst[:, u, :].rearrange("p (r d) -> p r d", r=R)).then_inc(s_xd[u], 16)
            sp.wait_ge(s_d, marks["rows"])
            sp.dma_start(yt.rearrange("(b p) w -> p b w", p=P), rows).then_inc(s_yt, 16)
            sp.wait_ge(s_d, marks["result"])
            sp.dma_start(out[0:(NB - 1) * P, :].rearrange("(b p) d -> p b d", p=P),
                         fin[:, 0:NB - 1, :]).then_inc(s_out, 16)
            sp.dma_start(out[(NB - 1) * P:N, :], fin[0:LAST, NB - 1, :]).then_inc(s_out, 16)
            sp.wait_ge(s_out, 32)

        @block.gpsimd
        def _(pool):
            nc_ = pool
            nc_.memset(ident[:, :], 0.0).then_inc(s_pool, 1)
            nc_.memset(ltri, 1.0).then_inc(s_pool, 1)
            nc_.memset(ones, 1.0).then_inc(s_pool, 1)
            nc_.iota(iota_r[:, :], pattern=[[1, P]], base=0, channel_multiplier=0,
                     allow_small_or_imprecise_dtypes=True).then_inc(s_pool, 1)
            nc_.iota(rowf[:, :], pattern=[[1, TW]], base=0, channel_multiplier=0,
                     allow_small_or_imprecise_dtypes=True).then_inc(s_pool, 1)
            pool.wait_ge(s_pool, 5)
            nc_.affine_select(out=ident[:, :], in_=ident[:, :], compare_op=ALU.not_equal, fill=1.0, base=0,
                              pattern=[[-1, P]], channel_multiplier=1).then_inc(s_pool, 1)
            nc_.affine_select(out=ltri, in_=ltri, compare_op=ALU.is_gt, fill=0.0, base=0,
                              pattern=[[1, P]], channel_multiplier=-1).then_inc(s_pool, 1)
            pool.wait_ge(s_pool, 7)
            nc_.tensor_copy(identb[:, :], ident[:, :]).then_inc(s_pool, 1)
            pool.wait_ge(s_fill, 16)
            with pool.Fori(0, ET // U) as i:
                for u in range(U):
                    if u % HALF == 0:
                        reg_wait(pool, s_sidx, i * 2 + (u // HALF + 1))
                    pool.indirect_dma_start(
                        out=table, out_offset=bass.IndirectOffsetOnAxis(ap=sring[:, u, 4:5], axis=0),
                        in_=sring[:, u, 0:PAYS], in_offset=None).then_inc(s_scat[u], 16)

            def gather(source, to, slot):
                pool.indirect_dma_start(
                    out=to[:, slot, :], out_offset=None, in_=source,
                    in_offset=bass.IndirectOffsetOnAxis(ap=idx[:, slot:slot + 1], axis=0),
                ).then_inc(s_g[slot], 16)

            for l in range(L):
                for u in range(XU):
                    pool.wait_ge(s_xd[u], 16 * (NB // XU) * (l + 1))
                with pool.Fori(0, NT // U) as i:
                    for u in range(U):
                        if u % HALF == 0:
                            pool.wait_ge(s_idx, i * (U // HALF) + (l * (NT // HALF + 2) + u // HALF + 1))
                            reg_wait(pool, s_used, i * U + (NT * l + u + HALF))
                        gather(xt, grow, u)
            pool.wait_ge(s_yt, 16)
            Q0 = LEAD * G // HALF
            for q in range(Q0):
                pool.wait_ge(s_idx, L * (NT // HALF + 2) + q + 1)
                pool.wait_ge(s_pv, 2 * q + 2)
                for u in range(HALF):
                    gather(yt, gat, (q * HALF + u) % RING)
            with pool.Fori(0, NG // SG) as i:
                for q in range(Q0, Q0 + RING // HALF):
                    pool.wait_ge(s_idx, i * (RING // HALF) + (L * (NT // HALF + 2) + q + 1))
                    reg_wait(pool, s_pv, i * SG + (2 * q + 2))
                    for u in range(HALF):
                        gather(yt, gat, (q * HALF + u) % RING)

        @block.tensor
        def _(pe):
            pe.wait_ge(s_pool, 8)
            pe.wait_ge(s_d, marks["counts"])
            pe.matmul(ps[:, 0, 0:NK], ltri, sm[:, 1, :], start=True, stop=True).then_inc(s_t, 1)
            pe.matmul(ps[:, 1, 0:NK], ones, sm[:, 1, :], start=True, stop=True).then_inc(s_t, 1)

            def turn(source):
                for b in range(NB):
                    mm = pe.transpose(ps[:, b // 4, (b % 4) * P:(b % 4 + 1) * P], source(b), ident[:, :])
                    if b % 4 == 3 or b == NB - 1:
                        mm.then_inc(s_t, 1)

            pe.wait_ge(s_const, 96)
            pe.wait_ge(s_d, marks["totals"])
            turn(lambda b: nodes[:, b, :])
            for l in range(L):
                pe.wait_ge(s_d, marks[f"features{l}"])
                with pe.Fori(0, NB // XU) as i:
                    for u in range(XU):
                        pe.wait_ge(s_hb, i * XU + (NB * l + u + 1))
                        for c in range(XC):
                            q = u * XC + c
                            pe.wait_ge(s_xe, i * (XU * XC) + (NB * XC * l + q + 1))
                            pe.matmul(ps[:, q % XB, 0:G3], hblk[:, u, :],
                                      wsb[:, l * R + 3 * c:l * R + 3 * c + 3, :].rearrange("p r d -> p (r d)"),
                                      start=True, stop=True).then_inc(s_xm, 1)
                pe.wait_ge(s_xe, XB + NB * XC * (l + 1))
                for c in range(7):
                    pe.matmul(ps[:, c, :], zerob[:, 0:P], zerob[:, :], start=True, stop=False,
                              skip_group_check=True)
                with pe.Fori(0, NT // U) as i:
                    for u in range(U):
                        if u % G == 0:
                            b = pe.value_load(blki[0:1, bass.ds(i * U + u, 1)], min_val=0, max_val=NB - 1)
                        pe.wait_ge(s_g[u], i * 16 + 16 * (NT // U * l + 1))
                        pe.wait_ge(s_oh, i * U + (NT * l + u + 1))
                        pe.matmul(agg[:, bass.ds(b * P, P)], grow[:, u, :], oh[:, u, :], start=False,
                                  stop=False, skip_group_check=True).then_inc(s_used, 1)
            pe.wait_ge(s_d, marks["sums"])
            turn(lambda b: hT[:, b * P:(b + 1) * P])
            pe.wait_ge(s_d, marks["rows"])
            turn(lambda b: rows[:, b, 0:D])
            pe.wait_ge(s_d, marks["turned"])

            def attend_step(k, j, on):
                later = k is not j
                if 0 in on:
                    for t in range(G):
                        slot, turns = (j * G + t) % RING, j * G // RING
                        base = 16 * (NT // U * L) if slot < U else 0
                        if later:
                            pe.wait_ge(s_g[slot], loop * 16 + (base + 16 * turns + 16))
                        else:
                            pe.wait_ge(s_g[slot], base + 16 * turns + 16)
                    if later or j >= 2:
                        pe.wait_ge(s_gt, k - 1)
                    for t in range(G):
                        mm = pe.transpose(ps[:, j % 2, t * P:(t + 1) * P], gat[:, (j * G + t) % RING, 0:D],
                                          ident[:, :])
                    mm.then_inc(s_tr, 1)
                if 1 in on:
                    v, s = k - 1, (j - 1) % 2
                    pe.wait_ge(s_gt, v + 1)
                    pe.wait_ge(s_ny, v * (G + 1) + (G + 1))
                    if later or j >= 3:
                        pe.wait_ge(s_ex, v * 2 - 2)
                    pe.matmul(ps[:, 2 + s, 0:GP], yb[:, s, :], gt[:, s, :], start=True, stop=False)
                    for t in range(G):
                        mm = pe.matmul(ps[:, 2 + s, t * P:(t + 1) * P], neg[:, s, t * P:(t + 1) * P],
                                       identb[:, :], start=False, stop=(t == G - 1))
                    mm.then_inc(s_sc, 1)
                if 3 in on:
                    v, s = k - 3, (j - 3) % 2
                    pe.wait_ge(s_ex, v * 2 + 1)
                    if later or j >= 5:
                        pe.wait_ge(s_pc, v - 1)
                    for t in range(G):
                        mm = pe.transpose(ps[:, 4 + s, t * P:(t + 1) * P], pr[:, s, t * P:(t + 1) * P],
                                          ident[:, :])
                    mm.then_inc(s_pt, 1)
                if 4 in on:
                    v, s = k - 4, (j - 4) % 2
                    pe.wait_ge(s_pc, v + 1)
                    if later or j >= 6:
                        pe.wait_ge(s_ac, v - 1)
                    for t in range(G):
                        mm = pe.matmul(ps[:, 6 + s, 0:D + 1], pt[:, s, t * P:(t + 1) * P],
                                       gat[:, ((j - 4) * G + t) % RING, D:2 * D + 1],
                                       start=(t == 0), stop=(t == G - 1))
                    mm.then_inc(s_pv, 1)

            for k in range(LEAD):
                attend_step(k, k, [t for t in (0, 1, 3, 4) if k >= t])
            with pe.Fori(0, NG // SG) as loop:
                for j in range(LEAD, LEAD + SG):
                    attend_step(loop * SG + j, j, [0, 1, 3, 4])
            for k in range(NG, NG + 4):
                attend_step(k, k - NG + LEAD + 2 * SG, [t for t in (1, 3, 4) if k - t < NG])

        @block.scalar
        def _(act):
            for l in range(L):
                act.wait_ge(s_d, marks[f"features{l}"])
                with act.Fori(0, NB // XU) as i:
                    for u in range(XU):
                        reg_wait(act, s_xm, i * (XU * XC) + (NB * XC * l + (u + 1) * XC))
                        act.copy(hblk[:, u, :], hT[:, bass.ds(i * (XU * P) + u * P, P)]).then_inc(s_hb, 1)
            act.wait_ge(s_d, marks["var0"])
            act.activation(mv[:, :, 1], mv[:, :, 1], ACT.Sqrt).then_inc(s_a, 1)
            act.wait_ge(s_d, marks["squares"])
            act.activation(sm[:, 10, 0:NB], sm[:, 9, 0:NB], ACT.Sqrt).then_inc(s_a, 1)
            act.wait_ge(s_d, marks["turned"])

            def attend_step(k, j, on):
                later = k is not j
                if 0 in on:
                    s = j % 2
                    act.wait_ge(s_tr, k + 1)
                    if later or j >= 2:
                        act.wait_ge(s_sc, k - 1)
                    act.activation(gt[:, s, :], ps[:, s, 0:GP], ACT.Copy).then_inc(s_gt, 1)
                if 2 in on:
                    v, s = k - 2, (j - 2) % 2
                    act.wait_ge(s_nm, v + 1)
                    if later or j >= 4:
                        act.wait_ge(s_pt, v - 1)
                    act.activation(pr[:, s, :], ps[:, 2 + s, 0:GP], ACT.Exp,
                                   bias=nmn[:, s:s + 1]).then_inc(s_ex, 1)
                    if later or j >= 6:
                        act.wait_ge(s_ac, v - 3)
                    act.activation(scl[:, (j - 2) % 4:(j - 2) % 4 + 1], nold[:, s:s + 1], ACT.Exp,
                                   bias=nmn[:, s:s + 1], scale=-1.0).then_inc(s_ex, 1)
                if 3 in on:
                    v, s = k - 3, (j - 3) % 2
                    act.wait_ge(s_pt, v + 1)
                    if later or j >= 5:
                        act.wait_ge(s_pv, v + (SG - 1))
                    act.activation(pt[:, s, :], ps[:, 4 + s, 0:GP], ACT.Copy).then_inc(s_pc, 1)

            for k in range(LEAD):
                attend_step(k, k, [t for t in (0, 2, 3) if k >= t])
            with act.Fori(0, NG // SG) as i:
                for j in range(LEAD, LEAD + SG):
                    attend_step(i * SG + j, j, [0, 2, 3])
            for k in range(NG, NG + 3):
                attend_step(k, k - NG + LEAD + 2 * SG, [t for t in (2, 3) if k - t < NG])
            act.wait_ge(s_d, marks["var2"])
            act.activation(mv[:, :, 1], mv[:, :, 1], ACT.Sqrt).then_inc(s_a, 1)


_INS = ['x', 'src', 'dst', 'edge_type_9', 'L0_gnn_weights', 'L0_gnn_biases', 'L1_gnn_beta']


def kernel(**inputs):
    import numpy as _np
    import concourse.bacc as _bacc
    from concourse import mybir as _mybir
    from concourse.bass_utils import run_bass_kernel_spmd as _run

    nc = _bacc.Bacc("TRN2", target_bir_lowering=False, num_devices=1)
    arrays, args = {}, []
    for name in _INS:
        a = _np.ascontiguousarray(inputs[name])
        arrays[f"in_{name}_dram"] = a
        args.append(nc.dram_tensor(f"in_{name}_dram", a.shape, _mybir.dt.from_np(a.dtype), kind="ExternalInput").ap())
    n, d = inputs['x'].shape
    args.append(nc.dram_tensor("out_0_dram", (n, d), _mybir.dt.float32, kind="ExternalOutput").ap())
    gnn_program(nc, *args)
    r = _run(nc, [arrays], core_ids=[0])
    return r.results[0]["out_0_dram"]
```

```python
from contextlib import ExitStack

import concourse.bass as bass
from concourse import mybir

F32 = mybir.dt.float32
BF16 = mybir.dt.bfloat16
F16 = mybir.dt.float16
I32 = mybir.dt.int32
I16 = mybir.dt.int16
ALU = mybir.AluOpType
ACT = mybir.ActivationFunctionType
AX = mybir.AxisListType

P = 128
U = 8
HALF = 4
G = 2
RING = 24
BIG = 1.0e30
EPS = 1e-05
SCAT = 16
KR = 4
ROW_BIT = 15
DIGIT = 11


def gnn_program(nc, x, src, dst, edge_type, weights, biases, beta, out):
    N, D = x.shape
    E = src.shape[0]
    L, R = weights.shape[0], weights.shape[1]
    NB = -(-N // P)
    NP = NB * P
    LAST = N - (NB - 1) * P
    RF = R * D
    ET = -(-E // (P * U)) * U
    FULL = E // ET
    REST = E - FULL * ET
    assert D == P and FULL == P - 1 and G == 2
    NK = NB + 1
    PAD_ROW = NB * P
    NT = -(-(E + NB * (P - 1)) // (P * U)) * U
    GP = G * P
    NA = -(-(E + NB * (GP - 1)) // GP * G // U) * U
    NG = NA // G
    TW = NA + RING
    assert (E + NB * (P - 1)) // P <= NT and (E + NB * (GP - 1)) // GP * G <= NA and NT % (2 * U) == 0
    INVALID = 64
    assert NB < INVALID
    SG = HALF // G
    SR = RING // HALF
    NS = NA // HALF
    LEAD = NS % SR + SR
    GP2 = SG * GP
    assert SG == 2 and RING % HALF == 0 and NA % HALF == 0 and SR % 2 == 0 and LEAD % 2 == 0
    CP = (ET // 2 + SCAT) // SCAT * SCAT
    EP = ET - CP
    HW = NT // 2
    BLOCK_SHIFT = 10
    BLOCK_MUL = -(-(1 << BLOCK_SHIFT) // NB)
    assert CP <= REST and EP % U == 0 and U == 2 * KR and HW <= 512 and NT <= 1 << DIGIT
    assert R * NP < 1 << ROW_BIT and ROW_BIT + 7 <= 2 * DIGIT
    assert all(b * BLOCK_MUL >> BLOCK_SHIFT == b // NB for b in range(R * NB))
    HL = 2 * D + 4
    G3 = 3 * D
    XC = RF // G3
    XB = 5
    XBANKS = [7, 0, 1, 2, 3]
    XU = 5
    assert NB % XU == 0 and RF % G3 == 0
    XN = NB // XU
    HC = -(-NG // P)
    BANKS = -(-NP // 512)
    PIECES = [[(c, max(512 * c, i * XU * P), min(512 * (c + 1), (i + 1) * XU * P)) for c in range(BANKS)
               if max(512 * c, i * XU * P) < min(512 * (c + 1), (i + 1) * XU * P)] for i in range(XN)]
    FREE = [-(-min(512 * (c + 1), NP) // (XU * P)) for c in range(BANKS)]
    assert BANKS == 7 and HC * P <= 512

    table = nc.dram_tensor("scattered_edges", (P * NT, 1), I32, kind="Internal").ap()
    xt = nc.dram_tensor("x_of_type", (R * NP, D), F32, kind="Internal").ap()
    yt = nc.dram_tensor("attended_rows", (NP, HL), F32, kind="Internal").ap()

    with ExitStack() as ctx:
        def sb(name, shape, dt=F32):
            return ctx.enter_context(nc.sbuf_tensor(name, shape, dt))

        def sem(name):
            return ctx.enter_context(nc.semaphore(name))

        nodes = sb("nodes", [P, NB, D])
        wsb = sb("wsb", [P, L * R, D])
        bias = sb("bias", [P, L * RF])
        hT = sb("hT", [P, NP])
        ident = sb("ident", [P, P])
        maskb = sb("maskb", [P, P], BF16)
        zerob = sb("zerob", [P, 512], BF16)
        iota_r = sb("iota_r", [P, P])
        tab = sb("tab", [P, NA], I32)
        gix = sb("gix", [P, TW], I32)
        nix = sb("nix", [P, TW], I32)
        rowf = sb("rowf", [P, TW])
        blk = sb("blk", [P, TW])
        iota_g = sb("iota_g", [P, NG])
        iota_h = sb("iota_h", [P, HC])
        endcol = sb("endcol", [P, 4])
        lastg = sb("lastg", [P, HC, NB])
        nogrp = sb("nogrp", [P, NB])
        fresh = sb("fresh", [P, NG])
        hist = sb("hist", [P, NG + 1])
        blkc = sb("blkc", [P, NG], I32)
        blka = sb("blka", [P, NG], I32)
        betab = sb("betab", [P, 1])
        idx = sb("idx", [P, RING], I32)
        oh = sb("oh", [P, U, P])
        sm = sb("sm", [P, 12, NK])
        smi = sb("smi", [P, 2, NK], I32)

        wide = sb("wide", [P, TW])
        blkt = sb("blkt", [P, NT], I32)
        words = sb("words", [P, NB + NA])
        shift = sb("shift", [P, NG, G])

        REGION = 25 * 1024
        region = sb("region", [P, REGION])
        used = [0]

        def part(words, dt=F32):
            a = region[:, used[0]:used[0] + words]
            used[0] += words
            assert used[0] <= REGION, used[0]
            return a if dt == F32 else a.bitcast(dt)

        eq = part(NK * ET // 2, BF16).rearrange("p (b t) -> p b t", b=NK)
        cum = part(NK * ET // 2, I16).rearrange("p (b t) -> p b t", b=NK)
        pay = part(CP * 2, I32).rearrange("p (t w) -> p t w", w=2)
        sring = part(SCAT * 2, I32).rearrange("p (t w) -> p t w", w=2)
        keyb = part(ET // 2, BF16)
        pos = part(ET)
        posi = part(ET, I32)
        word = part(ET, I32)
        iota_s = part(NT // 2, F16)
        used[0] = NK * ET // 2
        cols = part((EP + KR) * 4)
        few = part(2 * KR * 4).rearrange("p (h w) -> p h w", h=2)
        oh_q = part(KR * P, F16).rearrange("p (u d q) -> p u d q", u=KR, d=2)
        oh_s = part(KR * NT // 2, F16).rearrange("p (u s) -> p u s", u=KR)
        assert used[0] <= NK * ET
        most = max(CP, EP)
        tmps = (blk[:, 0:most], blk[:, most:2 * most], wide[:, 0:most], wide[:, most:2 * most])
        assert 2 * most <= TW
        srci, dsti, typei = (hT[:, n * ET:(n + 1) * ET].bitcast(I32) for n in range(3))
        used[0] = 0
        grow = part(U * D).rearrange("p (u d) -> p u d", u=U)
        hblk = part(XU * P).rearrange("p (u d) -> p u d", u=XU)
        xst = part(XU * RF).rearrange("p (u w) -> p u w", u=XU)
        used[0] = 0
        gat = part(RING * HL).rearrange("p (u w) -> p u w", u=RING)
        rows = part(NB * HL).rearrange("p (b w) -> p b w", b=NB)
        acc = part(NB * (D + 1)).rearrange("p (b w) -> p b w", b=NB)
        gt = part(2 * GP2).rearrange("p (s w) -> p s w", s=2)
        yb = part(2 * SG * P).rearrange("p (s w) -> p s w", s=2)
        neg = part(GP2, BF16).rearrange("p (s w) -> p s w", s=2)
        pr = part(2 * GP2).rearrange("p (s w) -> p s w", s=2)
        pt = part(2 * GP2).rearrange("p (s w) -> p s w", s=2)
        ntm = part(2 * SG).rearrange("p (s w) -> p s w", s=2)
        old = part(2 * SG).rearrange("p (s w) -> p s w", s=2)
        dif = part(2 * SG).rearrange("p (s w) -> p s w", s=2)
        scl = part(SR * SG).rearrange("p (s w) -> p s w", s=SR)
        fin = part(NB * D).rearrange("p (b w) -> p b w", b=NB)
        ltri, ones = oh[:, 0, :], oh[:, 1, :]

        stats = sb("stats", [P, NB, 6])
        mv = sb("mv", [P, NB, 2])
        selfm = sb("selfm", [P, NB])
        lastm = sb("lastm", [P, NB])
        fold = sb("fold", [P, 4, NB])

        ps = ctx.enter_context(nc.psum_tensor("ps", [P, 8, 512], F32))
        agg = ps[:, 0:7, :].rearrange("p k n -> p (k n)")

        s_edges = sem("s_edges")
        s_const = sem("s_const")
        s_pool = sem("s_pool")
        s_d = sem("s_d")
        s_a = sem("s_a")
        s_t = sem("s_t")
        s_fill = sem("s_fill")
        s_sidx = [sem(f"s_sidx{h}") for h in range(2)]
        s_scat = [sem(f"s_scat{u}") for u in range(SCAT)]
        s_few = sem("s_few")
        s_cell = sem("s_cell")
        s_put = sem("s_put")
        s_srt = sem("s_srt")
        s_feat = sem("s_feat")
        s_hb = sem("s_hb")
        s_mv = sem("s_mv")
        s_xm = sem("s_xm")
        s_xe = sem("s_xe")
        s_xd = [sem(f"s_xd{u}") for u in range(XU)]
        s_idx = sem("s_idx")
        s_g = [sem(f"s_g{u}") for u in range(RING)]
        s_oh = sem("s_oh")
        s_used = sem("s_used")
        s_pl = sem("s_pl")
        s_un = sem("s_un")
        s_se = sem("s_se")
        s_res = sem("s_res")
        s_yt = sem("s_yt")
        s_tr = sem("s_tr")
        s_gt = sem("s_gt")
        s_ny = sem("s_ny")
        s_sc = sem("s_sc")
        s_yb = sem("s_yb")
        s_mx = sem("s_mx")
        s_nm = sem("s_nm")
        s_od = sem("s_od")
        s_df = sem("s_df")
        s_ex = sem("s_ex")
        s_sl = sem("s_sl")
        s_pt = sem("s_pt")
        s_pc = sem("s_pc")
        s_pv = sem("s_pv")
        s_ac = sem("s_ac")
        s_out = sem("s_out")

        marks = {}

        block = ctx.enter_context(nc.Block())

        def block_of(eng, offsets, k, most, n=SG):
            return nc.values_load_multi_w_load_instructions(
                offsets[0:1, bass.ds(k * n, n)], engines=[eng.engine], min_val=0, max_val=most)[1]

        def reg_wait(eng, s, value):
            eng.wait_ge(s, value)
            eng.nop(nofuse=True)

        def store_x(eng, i, u):
            xv = xt.rearrange("(r n) d -> n r d", r=R)
            eng.dma_start(xv[bass.ds(i * (XU * P) + u * P, P), :, :],
                          xst[:, u, :].rearrange("p (r d) -> p r d", r=R)).then_inc(s_xd[u], 16)

        @block.vector
        def _(dve):
            steps = [0]

            def step(ins, mark=None):
                steps[0] += 1
                ins.then_inc(s_d, 1)
                dve.wait_ge(s_d, steps[0])
                if mark:
                    marks[mark] = steps[0]

            dve.sem_inc(s_used, U)
            dve.sem_inc(s_put, KR)
            dve.sem_inc(s_pv, SR)
            dve.sem_inc(s_xe, XB)
            dve.sem_inc(s_xm, XU * XC)
            nc_ = dve
            step(nc_.memset(srci, PAD_ROW))
            step(nc_.memset(dsti, 0))
            step(nc_.memset(typei, 0), "cleared")
            nc_.memset(zerob[:, :], 0.0)
            nc_.memset(words[:, 0:NB], 0.0)
            nc_.memset(words[:, NB + NT:NB + NA], 0.0)
            step(nc_.memset(wide[:, NA:TW], -1.0))
            step(nc_.memset(gix[:, NT:TW], 0))
            step(nc_.memset(nix[:, NA:TW], 0))
            step(nc_.memset(tab[:, :], 0), "filler")

            dve.wait_ge(s_edges, 96)
            step(nc_.tensor_scalar(posi, srci, 7, None, ALU.arith_shift_right))
            step(nc_.tensor_copy(keyb, posi))
            step(nc_.tensor_scalar(posi, posi, float(NB - 1), -float(P), ALU.min, ALU.mult))
            step(nc_.tensor_tensor(posi, srci, posi, ALU.add))
            step(nc_.scalar_tensor_tensor(out=word, in0=typei, scalar=float(NP), in1=dsti,
                                          op0=ALU.mult, op1=ALU.add))
            step(nc_.scalar_tensor_tensor(out=word, in0=posi, scalar=float(1 << ROW_BIT), in1=word,
                                          op0=ALU.mult, op1=ALU.add))
            step(nc_.tensor_scalar(word, word, 1.0, None, ALU.add))
            for b in range(NK):
                ins = nc_.tensor_scalar(eq[:, b, :], keyb, float(b), None, ALU.is_equal)
            step(ins)
            eqf = eq.rearrange("p b t -> p (b t)")
            step(nc_.tensor_tensor_scan(cum.rearrange("p b t -> p (b t)"), eqf, eqf, 0.0,
                                        ALU.add, ALU.bypass))
            ends, cnt, prev, pre, tot, til, te, ts, off = (sm[:, i, :] for i in range(9))
            step(nc_.tensor_copy(ends, cum[:, :, ET - 1]))
            step(nc_.memset(prev[:, 0:1], 0.0))
            step(nc_.tensor_copy(prev[:, 1:NK], ends[:, 0:NK - 1]))
            step(nc_.tensor_tensor(cnt, ends, prev, ALU.subtract), "counts")
            dve.wait_ge(s_t, 2)
            step(nc_.tensor_copy(pre, ps[:, 0, 0:NK]))
            step(nc_.tensor_copy(tot, ps[:, 1, 0:NK]), "totals")
            step(nc_.tensor_scalar(tot, tot, float(P - 1), None, ALU.add))
            step(nc_.tensor_copy(smi[:, 0, :], tot))
            step(nc_.tensor_scalar(smi[:, 1, :], smi[:, 0, :], 7, None, ALU.arith_shift_right))
            step(nc_.tensor_copy(til, smi[:, 1, :]))
            step(nc_.tensor_tensor_scan(te, til, til, 0.0, ALU.add, ALU.bypass))
            step(nc_.tensor_tensor(ts, te, til, ALU.subtract))
            step(nc_.scalar_tensor_tensor(out=off, in0=ts, scalar=float(P), in1=pre, op0=ALU.mult,
                                          op1=ALU.add))
            step(nc_.tensor_tensor(off, off, prev, ALU.subtract))
            step(nc_.tensor_scalar(off, off, -1.0, None, ALU.add))
            step(nc_.memset(pos, 0.0))

            def place(lo, n):
                def term(b):
                    nc_.scalar_tensor_tensor(out=tmps[b % 3][:, 0:n], in0=cum[:, b, lo:lo + n],
                                             scalar=off[:, b:b + 1], in1=eq[:, b, lo:lo + n],
                                             op0=ALU.add, op1=ALU.mult).then_inc(s_d, 1)
                    steps[0] += 1
                term(0)
                for b in range(NK):
                    before = steps[0]
                    if b + 1 < NK:
                        term(b + 1)
                    dve.wait_ge(s_d, before)
                    nc_.tensor_tensor(pos[:, lo:lo + n], pos[:, lo:lo + n], tmps[b % 3][:, 0:n],
                                      ALU.add).then_inc(s_d, 1)
                    steps[0] += 1
                dve.wait_ge(s_d, steps[0])
                step(nc_.tensor_copy(posi[:, lo:lo + n], pos[:, lo:lo + n]))

            place(0, CP)
            ti, tj = (t.bitcast(I32)[:, 0:CP] for t in tmps[0:2])
            step(nc_.tensor_scalar(ti, posi[:, 0:CP], P - 1, None, ALU.bitwise_and))
            step(nc_.tensor_scalar(tj, posi[:, 0:CP], 7, None, ALU.arith_shift_right))
            nc_.tensor_copy(pay[:, :, 0], word[:, 0:CP])
            step(nc_.scalar_tensor_tensor(out=pay[:, :, 1], in0=ti, scalar=float(NT), in1=tj,
                                          op0=ALU.mult, op1=ALU.add), "cells")
            tg, odd = sm[:, 9, :], sm[:, 10, :]
            step(nc_.tensor_scalar(smi[:, 0, :], smi[:, 1, :], 1, None, ALU.bitwise_and))
            step(nc_.tensor_copy(odd, smi[:, 0, :]))
            step(nc_.tensor_tensor(til, til, odd, ALU.add))
            step(nc_.tensor_scalar(til, til, 1.0 / G, None, ALU.mult))
            step(nc_.tensor_tensor_scan(tg, til, til, 0.0, ALU.add, ALU.bypass))
            dve.wait_ge(s_pool, 10)
            for n, a in enumerate((tg, te, odd)):
                step(nc_.tensor_tensor_reduce(out=sm[:, 11, :], in0=ident[:, 0:NK], in1=a, scale=1.0, scalar=0.0,
                                              op0=ALU.mult, op1=ALU.add, accum_out=endcol[:, n:n + 1]))
            step(nc_.tensor_scalar(endcol[:, 3:4], endcol[:, 0:1], -1.0, None, ALU.add))
            step(nc_.tensor_copy(te, tg))
            past_g, move, past_t = rowf[:, 0:NG], blk[:, 0:NG], gix[:, 0:NT].bitcast(F32)
            nc_.tensor_scalar(past_g, iota_g[:, :], endcol[:, 0:1], None, ALU.is_ge)
            nc_.tensor_scalar(past_t, iota_s, endcol[:, 1:2], None, ALU.is_ge)
            step(nc_.tensor_scalar(move, iota_g[:, :], endcol[:, 3:4], float(INVALID), ALU.is_equal, ALU.mult))
            step(nc_.tensor_tensor(move, move, past_g, ALU.add))
            step(nc_.tensor_scalar(move, move, endcol[:, 2:3], None, ALU.mult), "past")
            dve.wait_ge(s_t, 3)
            bg = hist[:, 1:NG + 1]
            step(nc_.tensor_copy(bg, ps[:, 7, 0:NG]))
            nc_.tensor_scalar(blkc[:, :], bg, float(P), None, ALU.mult)
            nc_.tensor_scalar(blka[:, :], bg, float(D + 1), None, ALU.mult)
            for n in range(2):
                nc_.tensor_scalar(blkt[:, n * HW:(n + 1) * HW], ps[:, 5 + n, 0:HW], float(P), None, ALU.mult)
            nc_.memset(hist[:, 0:1], BIG)
            nc_.tensor_copy(gix[:, 0:NG], ps[:, 4, 0:NG])
            step(nc_.tensor_scalar(shift[:, :, 1], ps[:, 4, 0:NG], -1.0, float(NB), ALU.mult, ALU.add))

            place(CP, EP)
            parts = [t.bitcast(I32)[:, 0:EP] for t in tmps]
            nc_.tensor_scalar(parts[0], posi[:, CP:ET], P - 1, None, ALU.bitwise_and)
            nc_.tensor_scalar(parts[1], posi[:, CP:ET], 7, None, ALU.arith_shift_right)
            nc_.tensor_scalar(parts[2], word[:, CP:ET], DIGIT, None, ALU.arith_shift_right)
            step(nc_.tensor_scalar(parts[3], word[:, CP:ET], (1 << DIGIT) - 1, None, ALU.bitwise_and))
            nc_.memset(cols[:, 4 * EP:], 0.0)
            for n in range(4):
                ins = nc_.tensor_copy(cols[:, 0:4 * EP].rearrange("p (t w) -> p t w", w=4)[:, :, n], parts[n])
            step(ins)

            def take_few(h, t):
                nc_.tensor_copy(few[:, h, :], cols[:, bass.ds(t * 4, KR * 4)]).then_inc(s_few, 1)

            take_few(0, 0)
            with dve.Fori(0, EP // U) as i:
                for u in range(U):
                    h, k = u // KR, u % KR
                    if k == 0:
                        dve.wait_ge(s_few, i * 2 + (h + 1))
                        dve.nop(nofuse=True)
                    q, s, high, low = (few[:, h, 4 * k + n:4 * k + n + 1] for n in range(4))
                    dve.wait_ge(s_put, i * U + (u + 1))
                    nc_.tensor_scalar(oh_q[:, k, 0, :], iota_s[:, 0:P], q, high, ALU.is_equal, ALU.mult)
                    nc_.tensor_scalar(oh_q[:, k, 1, :], iota_s[:, 0:P], q, low, ALU.is_equal, ALU.mult)
                    nc_.tensor_scalar(oh_s[:, k, :], iota_s, s, None, ALU.is_equal).then_inc(s_cell, 1)
                    if k == 1:
                        reg_wait(dve, s_cell, i * U + u)
                        take_few(1 - h, i * U + (h + 1) * KR)
            dve.wait_ge(s_put, KR + EP)
            for n in range(2):
                nc_.tensor_copy(wide[:, n * HW:(n + 1) * HW], ps[:, n, 0:HW]).then_inc(s_d, 1)
            steps[0] += 2
            dve.wait_ge(s_d, steps[0])
            for n in range(2):
                ins = nc_.scalar_tensor_tensor(out=wide[:, n * HW:(n + 1) * HW], in0=wide[:, n * HW:(n + 1) * HW],
                                               scalar=float(1 << DIGIT), in1=ps[:, 2 + n, 0:HW],
                                               op0=ALU.mult, op1=ALU.add)
            step(ins, "digits")

            def read_table():
                dve.wait_ge(s_srt, 16)
                g, v = gix[:, 0:NT], blk[:, 0:NT].bitcast(I32)
                step(nc_.tensor_tensor(words[:, NB:NB + NT], wide[:, 0:NT], tab[:, 0:NT], ALU.add))
                step(nc_.tensor_scalar(g, words[:, NB:NB + NT], -1.0, None, ALU.add))
                step(nc_.tensor_scalar(v, g, ROW_BIT, None, ALU.arith_shift_right))
                nc_.tensor_copy(rowf[:, 0:NT], v)
                step(nc_.tensor_scalar(g, g, (1 << ROW_BIT) - 1, None, ALU.bitwise_and))
                step(nc_.tensor_scalar(g, g, float(R * NP - 1), None, ALU.min))

            def move_tiles(i):
                reg_wait(dve, s_mv, i * 2 + 1)
                nc_.scalar_tensor_tensor(out=blk[:, 0:NA], in0=shift[:, :, :].rearrange("p g n -> p (g n)"),
                                         scalar=iota_g[:, bass.ds(i, 1)], in1=words[:, bass.ds(i, NA)],
                                         op0=ALU.is_equal, op1=ALU.mult).then_inc(s_mv, 1)
                reg_wait(dve, s_mv, i * 2 + 2)
                nc_.tensor_tensor(wide[:, 0:NA], wide[:, 0:NA], blk[:, 0:NA], ALU.add).then_inc(s_mv, 1)

            def find_nodes():
                g, v, w = blk[:, 0:NA].bitcast(I32), tab[:, :], nix[:, 0:NA]
                dve.wait_ge(s_mv, 2 * (NB + 1) + 1)
                step(nc_.tensor_scalar(g, wide[:, 0:NA], -1.0, None, ALU.add))
                step(nc_.tensor_scalar(v, g, ROW_BIT, None, ALU.arith_shift_right))
                nc_.tensor_copy(wide[:, 0:NA], v)
                step(nc_.tensor_scalar(g, g, (1 << ROW_BIT) - 1, None, ALU.bitwise_and))
                step(nc_.tensor_scalar(g, g, float(R * NP - 1), None, ALU.min))
                step(nc_.tensor_scalar(v, g, 7, None, ALU.arith_shift_right))
                step(nc_.tensor_scalar(w, v, float(BLOCK_MUL), None, ALU.mult))
                step(nc_.tensor_scalar(v, w, BLOCK_SHIFT, None, ALU.arith_shift_right))
                step(nc_.scalar_tensor_tensor(out=w, in0=v, scalar=-float(NP), in1=g,
                                              op0=ALU.mult, op1=ALU.add))

            def put_idx(source, lo, h):
                nc_.tensor_copy(idx[:, h * HALF:(h + 1) * HALF],
                                source[:, bass.ds(lo, HALF)]).then_inc(s_idx, 1)

            for l in range(L):
                if l:
                    dve.wait_ge(s_used, U + NT * l)
                for i in range(XN):
                    for c, lo, hi in PIECES[i]:
                        if l == 0:
                            dve.wait_ge(s_t, 3 + c + 1)
                            ins = nc_.tensor_copy(hT[:, lo:hi], agg[:, lo:hi])
                        else:
                            ins = nc_.tensor_scalar(hT[:, lo:hi], agg[:, lo:hi], 0.0, None, ALU.max)
                    ins.then_inc(s_feat, 1)
                if l == 0:
                    dve.wait_ge(s_const, 96)
                def take_x(i, first):
                    for u in range(XU):
                        if not first:
                            reg_wait(dve, s_xd[u], i * 16 + 16 * (NB // XU) * l)
                        for c in range(XC):
                            dve.wait_ge(s_xm, i * (XU * XC) + (XU * XC + NB * XC * l + u * XC + c + 1))
                            nc_.tensor_tensor(xst[:, u, c * G3:(c + 1) * G3], ps[:, XBANKS[(u * XC + c) % XB], 0:G3],
                                              bias[:, l * RF + c * G3:l * RF + (c + 1) * G3],
                                              ALU.add).then_inc(s_xe, 1)

                if l:
                    for u in range(XU):
                        dve.wait_ge(s_xd[u], 16 * (NB // XU) * l)
                take_x(0, True)
                with dve.Fori(1, NB // XU) as i:
                    take_x(i, False)
                if l == 0:
                    step(nc_.tensor_scalar(nix[:, 0:NG], gix[:, 0:NG], INVALID - 1, None, ALU.bitwise_and))
                    step(nc_.tensor_scalar(shift[:, :, 0], nix[:, 0:NG], -1.0, float(NB), ALU.mult, ALU.add))
                    step(nc_.tensor_tensor(fresh[:, 1:NG], bg[:, 1:NG], bg[:, 0:NG - 1], ALU.not_equal))
                    nc_.memset(fresh[:, 0:1], BIG)
                    step(nc_.tensor_scalar(fresh[:, 1:NG], fresh[:, 1:NG], 2 * BIG, -BIG, ALU.mult, ALU.add))
                    read_table()
                put_idx(gix, 0, 0)
                put_idx(gix, HALF, 1)
                if l == 0:
                    nc_.memset(wide[:, 0:NA], 0.0).then_inc(s_mv, 1)
                if l == 1:
                    find_nodes()

                def match(i, moving):
                    for u in range(U):
                        dve.wait_ge(s_used, i * U + (NT * l + u + 1))
                        nc_.tensor_scalar(oh[:, u, :], iota_r[:, :], rowf[:, bass.ds(i * U + u, 1)], None,
                                          ALU.is_equal).then_inc(s_oh, 1)
                        if u % HALF == HALF - 1:
                            reg_wait(dve, s_used, i * U + (U + NT * l + u + 1))
                            put_idx(gix, i * U + (U - HALF + u + 1), u // HALF)
                    if moving:
                        move_tiles(i)

                moves = NB + 1 if l == 0 else 0
                if moves:
                    with dve.Fori(0, moves) as i:
                        match(i, True)
                with dve.Fori(moves, NT // U) as i:
                    match(i, False)

            dve.wait_ge(s_used, U + NT * L)
            for i in range(XN):
                for c, lo, hi in PIECES[i]:
                    ins = nc_.tensor_copy(hT[:, lo:hi], agg[:, lo:hi])
                ins.then_inc(s_feat, 1)

            def moments(z, b):
                return nc_.bn_stats(stats[:, b, :], z[:, b, :])

            def gather_moments():
                for b in range(NB):
                    ins = nc_.bn_aggr(mv[:, b, :], stats[:, b, :])
                step(ins)

            T0 = 3 + 7
            nc_.memset(rows[:, :, 2 * D:HL], 1.0)
            for b in range(0, NB, 4):
                n = min(4, NB - b)
                dve.wait_ge(s_t, T0 + b // 4 + 1)
                ins = nc_.tensor_tensor(nodes[:, b:b + n, :].rearrange("p b d -> p (b d)"),
                                        nodes[:, b:b + n, :].rearrange("p b d -> p (b d)"),
                                        ps[:, b // 4, 0:n * P], ALU.add)
            step(ins, "added")
            for b in range(NB):
                ins = moments(nodes, b)
            step(ins)
            gather_moments()
            dev, rt = sm[:, 9, 0:NB], sm[:, 10, 0:NB]
            nc_.tensor_scalar(rt, mv[:, :, 1], float(D), None, ALU.mult)
            step(nc_.tensor_scalar(dev, mv[:, :, 1], EPS, None, ALU.add), "var0")
            dve.wait_ge(s_a, 1)
            nc_.reciprocal(mv[:, :, 1], dev)
            step(nc_.reciprocal(rt, rt))
            step(nc_.tensor_tensor(rt, rt, dev, ALU.mult), "lengths")
            for b in range(NB):
                ins = nc_.tensor_scalar(rows[:, b, D:2 * D], nodes[:, b, :], mv[:, b, 0:1], mv[:, b, 1:2],
                                        ALU.subtract, ALU.mult)
                if b % XU == XU - 1:
                    ins.then_inc(s_pl, 1)
            for q in range(4):
                put_idx(nix, q * HALF, q)
            ss = sm[:, 11, 0:NB]
            step(nc_.reciprocal(ss, rt))
            step(nc_.tensor_tensor(ss, ss, ss, ALU.mult))
            step(nc_.tensor_tensor(selfm[:, :], ss, rt, ALU.mult))
            step(nc_.tensor_tensor(selfm[:, :], selfm[:, :], rt, ALU.mult))
            step(nc_.tensor_scalar(selfm[:, :], selfm[:, :], betab[:, 0:1], -1.0, ALU.mult, ALU.mult))
            step(nc_.memset(acc, 0.0))
            te, til = sm[:, 6, 0:NB], sm[:, 5, 0:NB]
            step(nc_.tensor_scalar(te, te, -1.0, None, ALU.add))
            step(nc_.memset(te[:, NB - 1:NB], float(NG - 1)))
            for c in range(HC):
                nc_.tensor_scalar(lastg[:, c, :], te, iota_h[:, c:c + 1], None, ALU.is_equal)
            step(nc_.memset(til[:, NB - 1:NB], 1.0))
            step(nc_.tensor_scalar(til, til, 0.0, None, ALU.is_equal))
            step(nc_.tensor_scalar(nogrp[:, :], til, 2 * BIG, -BIG, ALU.mult, ALU.add))
            for b in range(0, NB, 4):
                n = min(4, NB - b)
                dve.wait_ge(s_t, T0 + 7 + b // 4 + 1)
                ins = nc_.tensor_scalar(hT[:, b * P:(b + n) * P], ps[:, b // 4, 0:n * P], betab[:, 0:1],
                                        None, ALU.mult)
            step(ins, "turned")

            def masks(k, s):
                nc_.tensor_tensor(
                    neg[:, s, :].rearrange("p (t r) -> p t r", t=HALF),
                    iota_r[:, :].unsqueeze(1).to_broadcast([P, HALF, P]),
                    wide[:, bass.ds(k * HALF, HALF)].unsqueeze(2).to_broadcast([P, HALF, P]),
                    ALU.not_equal).then_inc(s_ny, 1)

            masks(0, 0)

            def attend_step(k, j, on):
                s = j % 2
                later = k is not j
                v = k - 4

                def fold(g):
                    a = acc.rearrange("p b w -> p (b w)")[:, bass.ds(bs[g], D + 1)]
                    nc_.scalar_tensor_tensor(out=a, in0=a, scalar=scl[:, (j - 4) % SR, g:g + 1],
                                             in1=ps[:, 6 + s, g * GP:g * GP + D + 1],
                                             op0=ALU.mult, op1=ALU.add).then_inc(s_ac, 1)

                if 0 in on:
                    if later or j >= 1:
                        dve.wait_ge(s_sc, k)
                    masks(k + 1, 1 - s)
                if 4 in on:
                    bs = block_of(dve, blka, v, (NB - 1) * (D + 1))
                    dve.wait_ge(s_sl, v + 1)
                    if later or j >= 5:
                        dve.wait_ge(s_ac, v * SG)
                    reg_wait(dve, s_pv, v + (SR + 1))
                    fold(0)
                if 0 in on:
                    dve.wait_ge(s_sc, k + 1)
                    nc_.tensor_reduce(ntm[:, s, :], ps[:, 2 + s, :].rearrange("p (g e) -> p g e", g=SG),
                                      AX.X, ALU.max, negate=True).then_inc(s_mx, 1)
                if 4 in on:
                    reg_wait(dve, s_ac, v * SG + 1)
                    fold(1)
                if 0 in on:
                    reg_wait(dve, s_mx, k + 1)
                    new = hist[:, bass.ds(k * SG + 1, SG)]
                    was = hist[:, bass.ds(k * SG, 1)]
                    nc_.tensor_tensor_scan(new, fresh[:, bass.ds(k * SG, SG)], ntm[:, s, :], was,
                                           ALU.max, ALU.min).then_inc(s_nm, 1)
                    if later or j >= 2:
                        reg_wait(dve, s_tr, k - 1)
                    put_idx(nix, k * HALF + 4 * HALF, (j + 4) % SR)
                    reg_wait(dve, s_nm, k + 1)
                    nc_.tensor_tensor(old[:, s, :], hist[:, bass.ds(k * SG, SG)],
                                      fresh[:, bass.ds(k * SG, SG)], ALU.max).then_inc(s_od, 1)
                    if later or j >= 2:
                        dve.wait_ge(s_sl, k - 1)
                    reg_wait(dve, s_od, k + 1)
                    nc_.tensor_tensor(dif[:, s, :], new, old[:, s, :], ALU.subtract).then_inc(s_df, 1)

            for k in range(LEAD):
                attend_step(k, k, [t for t in (0, 4) if k >= t])
            with dve.Fori(0, (NS - LEAD) // SR) as i:
                for j in range(LEAD, LEAD + SR):
                    attend_step(i * SR + j, j, [0, 4])
            for k in range(NS, NS + 4):
                attend_step(k, k - NS + LEAD + 2 * SR, [4])

            dve.wait_ge(s_t, T0 + 7 + 7 + 2)
            step(nc_.tensor_tensor(lastm[:, :], nogrp[:, :], ps[:, 1, 0:NB], ALU.max))
            both, w_acc, w_self, den = (fold[:, n, :] for n in range(4))
            step(nc_.tensor_tensor(both, lastm[:, :], selfm[:, :], ALU.min))
            step(nc_.tensor_tensor(w_acc, both, lastm[:, :], ALU.subtract))
            step(nc_.tensor_tensor(w_self, both, selfm[:, :], ALU.subtract), "weights")
            dve.wait_ge(s_a, 3)
            step(nc_.tensor_tensor(den, acc[:, :, D], w_acc, ALU.mult))
            step(nc_.tensor_tensor(den, den, w_self, ALU.add))
            step(nc_.reciprocal(den, den))
            step(nc_.tensor_tensor(w_acc, w_acc, den, ALU.mult))
            step(nc_.tensor_tensor(w_self, w_self, den, ALU.mult))
            step(nc_.tensor_scalar(w_self, w_self, 1.0, None, ALU.add))
            marks["shares"] = steps[0]
            for i in range(XN + 1):
                if i < XN:
                    dve.wait_ge(s_se, i + 1)
                    for b in range(i * XU, (i + 1) * XU):
                        ins = nc_.scalar_tensor_tensor(out=fin[:, b, :], in0=acc[:, b, 0:D],
                                                       scalar=w_acc[:, b:b + 1], in1=fin[:, b, :],
                                                       op0=ALU.mult, op1=ALU.add)
                    ins.then_inc(s_d, 1)
                    steps[0] += 1
                if i:
                    dve.wait_ge(s_d, steps[0] - (i < XN))
                    for b in range((i - 1) * XU, i * XU):
                        ins = moments(fin, b)
            step(ins)
            gather_moments()
            step(nc_.tensor_scalar(mv[:, :, 1], mv[:, :, 1], EPS, None, ALU.add), "var2")
            dve.wait_ge(s_a, 4)
            step(nc_.reciprocal(mv[:, :, 1], mv[:, :, 1]))
            for b in range(NB):
                ins = nc_.tensor_scalar(fin[:, b, :], fin[:, b, :], mv[:, b, 0:1], mv[:, b, 1:2],
                                        ALU.subtract, ALU.mult)
                if b % XU == XU - 1:
                    ins.then_inc(s_res, 1)

        @block.sync
        def _(sp):
            sp.wait_ge(s_d, marks["cleared"])
            for a, t in ((src, srci), (dst, dsti), (edge_type, typei)):
                sp.dma_start(t[0:FULL, :], a[0:FULL * ET].rearrange("(p t) -> p t", t=ET)).then_inc(s_edges, 16)
                sp.dma_start(t[FULL:P, 0:REST], a[FULL * ET:E].rearrange("(p t) -> p t", p=1)).then_inc(s_edges, 16)
            sp.dma_start(nodes[:, 0:NB - 1, :],
                         x[0:(NB - 1) * P, :].rearrange("(b p) d -> p b d", p=P)).then_inc(s_const, 16)
            sp.dma_start(nodes[0:LAST, NB - 1, :], x[(NB - 1) * P:N, :]).then_inc(s_const, 16)
            sp.dma_start(nodes[LAST:P, NB - 1, :], x[0:P - LAST, :]).then_inc(s_const, 16)
            sp.dma_start(wsb[:, :, :], weights.rearrange("l r e f -> e (l r) f")).then_inc(s_const, 16)
            sp.dma_start(bias[:, :], biases.rearrange("l r f -> (l r f)").partition_broadcast(P)).then_inc(s_const, 16)
            sp.dma_start(betab[:, :], beta.partition_broadcast(P)).then_inc(s_const, 16)
            sp.wait_ge(s_d, marks["filler"])
            cells = table.rearrange("(p t) w -> p (t w)", p=P)
            sp.dma_start(cells, tab[:, 0:NT]).then_inc(s_fill, 16)
            sp.wait_ge(s_d, marks["cells"])
            for h in range(2):
                sp.dma_start(sring[:, h * SCAT // 2:(h + 1) * SCAT // 2, :],
                             pay[:, h * SCAT // 2:(h + 1) * SCAT // 2, :]).then_inc(s_sidx[h], 16)
            with sp.Fori(0, CP // SCAT - 1) as i:
                for h in range(2):
                    for u in range(h * SCAT // 2, (h + 1) * SCAT // 2):
                        reg_wait(sp, s_scat[u], i * 16 + 16)
                    sp.dma_start(sring[:, h * SCAT // 2:(h + 1) * SCAT // 2, :],
                                 pay[:, bass.ds(i * SCAT + (SCAT + h * SCAT // 2), SCAT // 2), :]
                                 ).then_inc(s_sidx[h], 16)
            for u in range(SCAT):
                sp.wait_ge(s_scat[u], 16 * (CP // SCAT))
            sp.dma_start(tab[:, 0:NT], cells).then_inc(s_srt, 16)
            for l in range(1, L):
                with sp.Fori(0, NB // XU) as i:
                    for u in range(XU):
                        sp.wait_ge(s_xe, i * (XU * XC) + (XB + NB * XC * l + (u + 1) * XC))
                        store_x(sp, i, u)
            yv = yt.rearrange("(b p) w -> p b w", p=P)
            for i in range(XN):
                sp.wait_ge(s_un, i + 1)
                sp.dma_start(yv[:, i * XU:(i + 1) * XU, :], rows[:, i * XU:(i + 1) * XU, :]).then_inc(s_yt, 16)
            for i in range(XN):
                sp.wait_ge(s_res, i + 1)
                lo, hi = i * XU, min((i + 1) * XU, NB - 1)
                sp.dma_start(out[lo * P:hi * P, :].rearrange("(b p) d -> p b d", p=P),
                             fin[:, lo:hi, :]).then_inc(s_out, 16)
            sp.dma_start(out[(NB - 1) * P:N, :], fin[0:LAST, NB - 1, :]).then_inc(s_out, 16)
            sp.wait_ge(s_out, 16 * (XN + 1))

        @block.gpsimd
        def _(pool):
            nc_ = pool
            nc_.memset(ident[:, :], 0.0).then_inc(s_pool, 1)
            nc_.memset(ltri, 1.0).then_inc(s_pool, 1)
            nc_.memset(ones, 1.0).then_inc(s_pool, 1)
            nc_.iota(iota_r[:, :], pattern=[[1, P]], base=0, channel_multiplier=0,
                     allow_small_or_imprecise_dtypes=True).then_inc(s_pool, 1)
            nc_.iota(iota_g[:, :], pattern=[[1, NG]], base=0, channel_multiplier=0,
                     allow_small_or_imprecise_dtypes=True).then_inc(s_pool, 1)
            nc_.iota(iota_h[:, :], pattern=[[P, HC]], base=0, channel_multiplier=1,
                     allow_small_or_imprecise_dtypes=True).then_inc(s_pool, 1)
            nc_.iota(iota_s, pattern=[[1, NT]], base=0, channel_multiplier=0,
                     allow_small_or_imprecise_dtypes=True).then_inc(s_pool, 1)
            pool.wait_ge(s_pool, 7)
            nc_.affine_select(out=ident[:, :], in_=ident[:, :], compare_op=ALU.not_equal, fill=1.0, base=0,
                              pattern=[[-1, P]], channel_multiplier=1).then_inc(s_pool, 1)
            nc_.affine_select(out=ltri, in_=ltri, compare_op=ALU.is_gt, fill=0.0, base=0,
                              pattern=[[1, P]], channel_multiplier=-1).then_inc(s_pool, 1)
            pool.wait_ge(s_pool, 9)
            nc_.tensor_scalar(maskb[:, :], ident[:, :], -BIG, None, ALU.mult).then_inc(s_pool, 1)
            pool.wait_ge(s_fill, 16)
            with pool.Fori(0, CP // SCAT) as i:
                for u in range(SCAT):
                    if u % (SCAT // 2) == 0:
                        reg_wait(pool, s_sidx[u * 2 // SCAT], i * 16 + 16)
                    pool.indirect_dma_start(
                        out=table, out_offset=bass.IndirectOffsetOnAxis(ap=sring[:, u, 1:2], axis=0),
                        in_=sring[:, u, 0:1], in_offset=None).then_inc(s_scat[u], 16)

            def gather(source, to, slot):
                pool.indirect_dma_start(
                    out=to[:, slot, :], out_offset=None, in_=source,
                    in_offset=bass.IndirectOffsetOnAxis(ap=idx[:, slot:slot + 1], axis=0),
                ).then_inc(s_g[slot], 16)

            for l in range(L):
                for u in range(XU):
                    pool.wait_ge(s_xd[u], 16 * (NB // XU) * (l + 1))
                with pool.Fori(0, NT // U) as i:
                    for u in range(U):
                        if u % HALF == 0:
                            pool.wait_ge(s_idx, i * (U // HALF) + (l * (NT // HALF + 2) + u // HALF + 1))
                            reg_wait(pool, s_used, i * U + (NT * l + u + HALF))
                        gather(xt, grow, u)
            pool.wait_ge(s_yt, 16 * XN)
            for q in range(LEAD):
                pool.wait_ge(s_idx, L * (NT // HALF + 2) + q + 1)
                pool.wait_ge(s_pv, q + 1)
                for u in range(HALF):
                    gather(yt, gat, (q * HALF + u) % RING)
            with pool.Fori(0, (NS - LEAD) // SR) as i:
                for q in range(LEAD, LEAD + SR):
                    pool.wait_ge(s_idx, i * SR + (L * (NT // HALF + 2) + q + 1))
                    reg_wait(pool, s_pv, i * SR + (q + 1))
                    for u in range(HALF):
                        gather(yt, gat, (q * HALF + u) % RING)

        @block.tensor
        def _(pe):
            pe.wait_ge(s_pool, 10)
            pe.wait_ge(s_d, marks["counts"])
            pe.matmul(ps[:, 0, 0:NK], ltri, sm[:, 1, :], start=True, stop=True).then_inc(s_t, 1)
            pe.matmul(ps[:, 1, 0:NK], ones, sm[:, 1, :], start=True, stop=True).then_inc(s_t, 1)
            pe.wait_ge(s_d, marks["past"])
            pe.matmul(ps[:, 7, 0:NG], ones[0:NB - 1, :], rowf[0:NB - 1, 0:NG], start=True, stop=True)
            past_t = gix[:, 0:NT].bitcast(F32)
            for n in range(2):
                pe.matmul(ps[:, 5 + n, 0:HW], ones[0:NB - 1, :], past_t[0:NB - 1, n * HW:(n + 1) * HW],
                          start=True, stop=True)
            pe.matmul(ps[:, 4, 0:NG], ones[0:NB, :], blk[0:NB, 0:NG], start=True, stop=True).then_inc(s_t, 1)

            def turn(source, ready=None):
                for b in range(NB):
                    if ready and b % 4 == 0:
                        ready(b // 4)
                    mm = pe.transpose(ps[:, b // 4, (b % 4) * P:(b % 4 + 1) * P], source(b), ident[:, :])
                    if b % 4 == 3 or b == NB - 1:
                        mm.then_inc(s_t, 1)

            pe.wait_ge(s_d, marks["totals"])
            for c in range(4):
                pe.matmul(ps[:, c, :], zerob[:, 0:P], zerob[:, :], start=True, stop=False,
                          skip_group_check=True)
            with pe.Fori(0, EP // U) as i:
                for u in range(U):
                    k = u % KR
                    pe.wait_ge(s_cell, i * U + (u + 1))
                    for d in range(2):
                        for n in range(2):
                            mm = pe.matmul(ps[:, 2 * d + n, 0:HW], oh_q[:, k, d, :],
                                           oh_s[:, k, n * HW:(n + 1) * HW], start=False, stop=False,
                                           skip_group_check=True)
                    mm.then_inc(s_put, 1)

            pe.wait_ge(s_const, 96)
            pe.wait_ge(s_d, marks["digits"])
            turn(lambda b: nodes[:, b, :])
            for l in range(L):
                with pe.Fori(0, NB // XU) as i:
                    for u in range(XU):
                        pe.wait_ge(s_hb, i * XU + (NB * l + u + 1))
                        for c in range(XC):
                            q = u * XC + c
                            pe.wait_ge(s_xe, i * (XU * XC) + (NB * XC * l + q + 1))
                            if 0 < q < XB:
                                pe.wait_ge(s_feat, XN * l + FREE[XBANKS[q]])
                            pe.matmul(ps[:, XBANKS[q % XB], 0:G3], hblk[:, u, :],
                                      wsb[:, l * R + 3 * c:l * R + 3 * c + 3, :].rearrange("p r d -> p (r d)"),
                                      start=True, stop=True).then_inc(s_xm, 1)
                pe.wait_ge(s_xe, XB + NB * XC * (l + 1))
                for c in range(7):
                    pe.matmul(ps[:, c, :], zerob[:, 0:P], zerob[:, :], start=True, stop=False,
                              skip_group_check=True)
                with pe.Fori(0, NT // U) as i:
                    for u in range(U):
                        if u % HALF == 0:
                            bs = block_of(pe, blkt, i * (U // HALF) + u // HALF, (NB - 1) * P, HALF)
                        pe.wait_ge(s_g[u], i * 16 + 16 * (NT // U * l + 1))
                        pe.wait_ge(s_oh, i * U + (NT * l + u + 1))
                        pe.matmul(agg[:, bass.ds(bs[u % HALF], P)], grow[:, u, :], oh[:, u, :], start=False,
                                  stop=False, skip_group_check=True).then_inc(s_used, 1)
            turn(lambda b: hT[:, b * P:(b + 1) * P], lambda c: pe.wait_ge(s_feat, XN * L + FREE[c]))
            pe.wait_ge(s_d, marks["added"])
            turn(lambda b: rows[:, b, 0:D], lambda c: pe.wait_ge(s_un, FREE[c]))
            pe.wait_ge(s_d, marks["turned"])

            def attend_step(k, j, on):
                s = j % 2
                later = k is not j
                if 0 in on:
                    for t in range(HALF):
                        slot, turns = (j * HALF + t) % RING, j // SR
                        landed = 16 * (NT // U * L if slot < U else 0) + 16 * turns + 16
                        pe.wait_ge(s_g[slot], loop * 16 + landed if later else landed)
                    if later or j >= 2:
                        pe.wait_ge(s_gt, k - 1)
                    for t in range(HALF):
                        mm = pe.transpose(ps[:, s, t * P:(t + 1) * P], gat[:, (j * HALF + t) % RING, 0:D],
                                          ident[:, :])
                    mm.then_inc(s_tr, 1)
                if 2 in on:
                    v = k - 2
                    pe.wait_ge(s_ex, v + 1)
                    if later or j >= 4:
                        pe.wait_ge(s_pc, v - 1)
                    for t in range(HALF):
                        mm = pe.transpose(ps[:, 4 + s, t * P:(t + 1) * P], pr[:, s, t * P:(t + 1) * P],
                                          ident[:, :])
                    mm.then_inc(s_pt, 1)
                if 3 in on:
                    v = k - 3
                    pe.wait_ge(s_pc, v + 1)
                    if later or j >= 5:
                        pe.wait_ge(s_ac, v * SG - SG)
                    for t in range(HALF):
                        g = t // G
                        mm = pe.matmul(ps[:, 7 - s, g * GP:g * GP + D + 1],
                                       pt[:, 1 - s, t * P:(t + 1) * P],
                                       gat[:, ((j - 3) * HALF + t) % RING, D:2 * D + 1],
                                       start=(t % G == 0), stop=(t % G == G - 1))
                    mm.then_inc(s_pv, 1)
                if 0 in on:
                    pe.wait_ge(s_gt, k + 1)
                    pe.wait_ge(s_yb, k + 1)
                    pe.wait_ge(s_ny, k + 1)
                    if later or j >= 2:
                        pe.wait_ge(s_ex, k - 1)
                    for g in range(SG):
                        pe.matmul(ps[:, 2 + s, g * GP:(g + 1) * GP], yb[:, s, g * P:(g + 1) * P],
                                  gt[:, s, g * GP:(g + 1) * GP], start=True, stop=False)
                        for t in range(g * G, (g + 1) * G):
                            mm = pe.matmul(ps[:, 2 + s, t * P:(t + 1) * P], neg[:, s, t * P:(t + 1) * P],
                                           maskb[:, :], start=False, stop=(t % G == G - 1))
                    mm.then_inc(s_sc, 1)

            for k in range(LEAD):
                attend_step(k, k, [t for t in (0, 2, 3) if k >= t])
            with pe.Fori(0, (NS - LEAD) // SR) as loop:
                for j in range(LEAD, LEAD + SR):
                    attend_step(loop * SR + j, j, [0, 2, 3])
            for k in range(NS, NS + 3):
                attend_step(k, k - NS + LEAD + 2 * SR, [t for t in (2, 3) if k - t < NS])

            pe.wait_ge(s_nm, NS)
            pe.wait_ge(s_gt, NS)
            widths = [min(P, NG - c * P) for c in range(HC)]
            for c, n in enumerate(widths):
                mm = pe.transpose(ps[0:n, 0, c * P:(c + 1) * P], hist[:, 1 + c * P:1 + c * P + n], ident[:, :])
            mm.then_inc(s_t, 1)
            pe.wait_ge(s_a, 2)
            for c, n in enumerate(widths):
                mm = pe.matmul(ps[:, 1, 0:NB], gt[0:n, 0, c * P:(c + 1) * P], lastg[0:n, c, :],
                               start=(c == 0), stop=(c == HC - 1))
            mm.then_inc(s_t, 1)

        @block.scalar
        def _(act):
            for l in range(L):
                with act.Fori(0, NB // XU) as i:
                    reg_wait(act, s_feat, i + (XN * l + 1))
                    for u in range(XU):
                        reg_wait(act, s_xm, i * (XU * XC) + (NB * XC * l + (u + 1) * XC))
                        act.copy(hblk[:, u, :], hT[:, bass.ds(i * (XU * P) + u * P, P)]).then_inc(s_hb, 1)
                    if l == 0:
                        for u in range(XU):
                            reg_wait(act, s_xe, i * (XU * XC) + (XB + (u + 1) * XC))
                            store_x(act, i, u)
            act.wait_ge(s_d, marks["var0"])
            act.activation(sm[:, 9:11, 0:NB], sm[:, 9:11, 0:NB], ACT.Sqrt).then_inc(s_a, 1)
            act.wait_ge(s_d, marks["lengths"])
            for i in range(XN):
                act.wait_ge(s_pl, i + 1)
                for b in range(i * XU, (i + 1) * XU):
                    ins = act.activation(rows[:, b, 0:D], rows[:, b, D:2 * D], ACT.Copy,
                                         scale=sm[:, 10, b:b + 1])
                ins.then_inc(s_un, 1)
            act.wait_ge(s_d, marks["turned"])

            def attend_step(k, j, on):
                s = j % 2
                later = k is not j
                if 0 in on:
                    bs = block_of(act, blkc, k, (NB - 1) * P)
                    if later or j >= 2:
                        reg_wait(act, s_sc, k - 1)
                    for g in range(SG):
                        ins = act.copy(yb[:, s, g * P:(g + 1) * P], hT[:, bass.ds(bs[g], P)])
                    ins.then_inc(s_yb, 1)
                    act.wait_ge(s_tr, k + 1)
                    act.activation(gt[:, s, :], ps[:, s, :], ACT.Copy).then_inc(s_gt, 1)
                if 2 in on:
                    v = k - 2
                    act.wait_ge(s_pt, v + 1)
                    if later or j >= 4:
                        act.wait_ge(s_pv, v + (SR - 1))
                    act.activation(pt[:, s, :], ps[:, 4 + s, :], ACT.Copy).then_inc(s_pc, 1)
                if 1 in on:
                    v = k - 1
                    if later or j >= 3:
                        act.wait_ge(s_pt, v - 1)
                    reg_wait(act, s_nm, v + 1)
                    for g in range(SG):
                        ins = act.activation(pr[:, 1 - s, g * GP:(g + 1) * GP],
                                             ps[:, 3 - s, g * GP:(g + 1) * GP], ACT.Exp,
                                             bias=hist[:, bass.ds(v * SG + (g + 1), 1)])
                    ins.then_inc(s_ex, 1)
                    if later or j >= SR + 1:
                        act.wait_ge(s_ac, v * SG - (SR - 1) * SG)
                    act.wait_ge(s_df, v + 1)
                    act.activation(scl[:, (j - 1) % SR, :], dif[:, 1 - s, :], ACT.Exp).then_inc(s_sl, 1)

            for k in range(LEAD):
                attend_step(k, k, [t for t in (0, 1, 2) if k >= t])
            with act.Fori(0, (NS - LEAD) // SR) as i:
                for j in range(LEAD, LEAD + SR):
                    attend_step(i * SR + j, j, [0, 1, 2])
            for k in range(NS, NS + 2):
                attend_step(k, k - NS + LEAD + 2 * SR, [t for t in (1, 2) if k - t < NS])
            act.wait_ge(s_sc, NS)
            act.wait_ge(s_t, 3 + 7 + 7 + 7 + 1)
            rest = NG - (HC - 1) * P
            act.copy(gt[:, 0, 0:(HC - 1) * P], ps[:, 0, 0:(HC - 1) * P])
            act.copy(gt[0:rest, 0, (HC - 1) * P:HC * P], ps[0:rest, 0, (HC - 1) * P:HC * P]).then_inc(s_a, 1)
            act.wait_ge(s_d, marks["weights"])
            act.activation(fold[:, 1:3, :], fold[:, 1:3, :], ACT.Exp).then_inc(s_a, 1)
            act.wait_ge(s_d, marks["shares"])
            for i in range(XN):
                for b in range(i * XU, (i + 1) * XU):
                    ins = act.activation(fin[:, b, :], rows[:, b, D:2 * D], ACT.Copy, scale=fold[:, 2, b:b + 1])
                ins.then_inc(s_se, 1)
            act.wait_ge(s_d, marks["var2"])
            act.activation(mv[:, :, 1], mv[:, :, 1], ACT.Sqrt).then_inc(s_a, 1)


_INS = ['x', 'src', 'dst', 'edge_type_9', 'L0_gnn_weights', 'L0_gnn_biases', 'L1_gnn_beta']


def kernel(**inputs):
    import numpy as _np
    import concourse.bacc as _bacc
    from concourse import mybir as _mybir
    from concourse.bass_utils import run_bass_kernel_spmd as _run

    nc = _bacc.Bacc("TRN2", target_bir_lowering=False, num_devices=1)
    arrays, args = {}, []
    for name in _INS:
        a = _np.ascontiguousarray(inputs[name])
        arrays[f"in_{name}_dram"] = a
        args.append(nc.dram_tensor(f"in_{name}_dram", a.shape, _mybir.dt.from_np(a.dtype), kind="ExternalInput").ap())
    n, d = inputs['x'].shape
    args.append(nc.dram_tensor("out_0_dram", (n, d), _mybir.dt.float32, kind="ExternalOutput").ap())
    gnn_program(nc, *args)
    r = _run(nc, [arrays], core_ids=[0])
    return r.results[0]["out_0_dram"]
```
